# Optimizing a Trainium2 kernel written in Bass

```python
import numpy as np
import jax
import jax.numpy as jnp

def _softmax(x, axis=-1):
    return jax.nn.softmax(x, axis=axis)

def _gelu(x):
    return jax.nn.gelu(x, approximate=True)

def _silu(x):
    return jax.nn.silu(x)

def _sigmoid(x):
    return jax.nn.sigmoid(x)

def _layernorm(x, axis=-1, eps=1e-05):
    m = jnp.mean(x, axis=axis, keepdims=True)
    v = jnp.var(x, axis=axis, keepdims=True)
    return (x - m) / jnp.sqrt(v + eps)

def _scatter_add(tgt, idx, src, axis=0):
    return tgt.at[idx].add(src)

def _segment_sum(src, seg, n):
    return jax.ops.segment_sum(src, seg, n)
kernel_name = 'mk_flamingo_gated_d1_seqx_r2_3672cd'

def setup_inputs(seed: int=0):
    np.random.seed(seed)
    _w = jnp.asarray

    def _rec_inputs():
        import jax
        import jax.numpy as jnp
        _rk = jax.random.key(seed)
        x = -0.0003929 + 0.9999 * jax.random.normal(jax.random.fold_in(_rk, 1), (8, 512, 512), jnp.float32)
        _lenS = 512 - jax.random.randint(jax.random.fold_in(_rk, 7), (8,), 0, max(1, 512 // 4) + 1, jnp.int32)
        _lenS2 = 512 - jax.random.randint(jax.random.fold_in(_rk, 8), (8,), 0, max(1, 512 // 4) + 1, jnp.int32)
        _ctx_1024P = jax.random.normal(jax.random.fold_in(_rk, 11), (8, 16, 512), jnp.float32)
        _ctx_1024c = jax.random.dirichlet(jax.random.fold_in(_rk, 511), 0.3 * jnp.ones((16,), jnp.float32), (8, 512))
        _ctx_1024t = jnp.einsum('bsk,bkd->bsd', _ctx_1024c, _ctx_1024P)
        _ctx_1024t = _ctx_1024t * jax.lax.rsqrt(jnp.mean(jnp.square(_ctx_1024t)) + 1e-12) * 0.953939
        ctx_1024 = 2.81802e-05 + 1.00001 * (_ctx_1024t + 0.3 * jax.random.normal(jax.random.fold_in(_rk, 611), (8, 512, 512), jnp.float32))
        _validS = jnp.arange(512)[None, :] < _lenS[:, None]
        _validS2 = jnp.arange(512)[None, :] < _lenS2[:, None]
        _causal = jnp.tril(jnp.ones((512, 512), dtype=bool))
        mask_BxS2_ik1 = jnp.where(jnp.broadcast_to(_validS2[:, :], (8, 512)), 1, 0).astype(jnp.int32)
        _g = jax.random.normal(jax.random.fold_in(_rk, 9001), (2, 1), jnp.float32)
        _g = jnp.sign(_g) * jnp.maximum(jnp.abs(_g), 1.0) + (_g == 0) * 1.0
        g_xattn = _g[0]
        g_ffn = _g[1]
        return (x, ctx_1024, mask_BxS2_ik1, g_xattn, g_ffn)
    x, ctx_1024, mask_BxS2_ik1, g_xattn, g_ffn = _rec_inputs()

    def _L0_xattn_setup():
        import jax, jax.numpy as jnp
        import numpy as np
        MASK_FILL = -99999.0
        key = jax.random.key(seed)
        k1, k2, k3, k4, k5, k6, k7 = jax.random.split(key, 7)
        B, S, H = (8, 1024, 512)
        query = jax.random.normal(k1, (B, S, H), dtype=jnp.float32)
        key_t = jax.random.normal(k2, (B, S, H), dtype=jnp.float32)
        value = jax.random.normal(k3, (B, S, H), dtype=jnp.float32)
        mask = jax.random.randint(k4, (B, S), 0, 2, dtype=jnp.int32)
        s = 1.0 / np.sqrt(H)
        Wq = jax.random.uniform(k5, (H, H), dtype=jnp.float32, minval=-s, maxval=s)
        Wk = jax.random.uniform(k6, (H, H), dtype=jnp.float32, minval=-s, maxval=s)
        Wv = jax.random.uniform(k7, (H, H), dtype=jnp.float32, minval=-s, maxval=s)
        return {'query': query, 'key': key_t, 'value': value, 'Wq': Wq, 'Wk': Wk, 'Wv': Wv, 'mask': mask}
    _L0_xattn_all = _L0_xattn_setup()
    _L0_xattn_in = {k: v for k, v in _L0_xattn_all.items() if k in ('Wq', 'Wk', 'Wv')}
    del _L0_xattn_all

    def _L0_ffn_setup():
        import jax, jax.numpy as jnp
        import numpy as np
        key = jax.random.key(seed)
        ks = jax.random.split(key, 5)
        B, S, D_in, D_out, E, R = (4, 512, 512, 512, 8, 16)
        x = jax.random.normal(ks[0], (B, S, D_in), dtype=jnp.float32)
        weight = jax.random.normal(ks[1], (D_out, D_in), dtype=jnp.float32) / np.sqrt(D_in)
        gate_w = jax.random.normal(ks[2], (E, D_in), dtype=jnp.float32) / np.sqrt(D_in)
        lora_U = jax.random.normal(ks[3], (E, R, D_in), dtype=jnp.float32) / np.sqrt(D_in)
        lora_V = jax.random.normal(ks[4], (E, D_out, R), dtype=jnp.float32) / np.sqrt(R)
        return {'x': x, 'weight': weight, 'gate_w': gate_w, 'lora_U': lora_U, 'lora_V': lora_V}
    _L0_ffn_all = _L0_ffn_setup()
    _L0_ffn_in = {k: v for k, v in _L0_ffn_all.items() if k in ('weight', 'gate_w', 'lora_U', 'lora_V')}
    del _L0_ffn_all
    return {'x': x, 'ctx_1024': ctx_1024, 'mask_BxS2_ik1': mask_BxS2_ik1, 'g_xattn': g_xattn, 'g_ffn': g_ffn, 'L0_xattn_Wq': _L0_xattn_in['Wq'], 'L0_xattn_Wk': _L0_xattn_in['Wk'], 'L0_xattn_Wv': _L0_xattn_in['Wv'], 'L0_ffn_weight': _L0_ffn_in['weight'], 'L0_ffn_gate_w': _L0_ffn_in['gate_w'], 'L0_ffn_lora_U': _L0_ffn_in['lora_U'], 'L0_ffn_lora_V': _L0_ffn_in['lora_V']}

def reference(x, ctx_1024, mask_BxS2_ik1, g_xattn, g_ffn, L0_xattn_Wq, L0_xattn_Wk, L0_xattn_Wv, L0_ffn_weight, L0_ffn_gate_w, L0_ffn_lora_U, L0_ffn_lora_V):
    import jax
    import jax.numpy as jnp

    def _L0_xattn_ref(query, key, value, Wq, Wk, Wv, mask):
        import jax, jax.numpy as jnp
        import numpy as np
        MASK_FILL = -99999.0
        q = jnp.einsum('bsh,oh->bso', query, Wq)
        k = jnp.einsum('bsh,oh->bso', key, Wk)
        v = jnp.einsum('bsh,oh->bso', value, Wv)
        score = jnp.einsum('bqh,bkh->bqk', q, k)
        m = mask[:, None, :]
        score = jnp.where(m == 0, jnp.float32(MASK_FILL), score)
        attn = jax.nn.softmax(score, axis=-1)
        context = jnp.einsum('bqk,bkh->bqh', attn, v)
        return context

    def _L0_ffn_ref(x, weight, gate_w, lora_U, lora_V):
        import jax, jax.numpy as jnp
        import numpy as np
        scaling = 1.0 / lora_U.shape[1]
        B, S, D_in = x.shape
        xt = x.reshape(-1, D_in)
        gate = jax.nn.softmax(xt @ gate_w.T, axis=-1)
        base = xt @ weight.T
        t = jnp.einsum('nh,erh->ner', xt, lora_U)
        lora = jnp.einsum('ne,eor,ner->no', gate, lora_V, t)
        out = base + scaling * lora
        return out.reshape(B, S, -1)
    x = x + jnp.tanh(g_xattn[0]) * _L0_xattn_ref(_layernorm(x, axis=-1), ctx_1024, ctx_1024, L0_xattn_Wq, L0_xattn_Wk, L0_xattn_Wv, mask_BxS2_ik1)
    x = x + jnp.tanh(g_ffn[0]) * _L0_ffn_ref(_layernorm(x, axis=-1), L0_ffn_weight, L0_ffn_gate_w, L0_ffn_lora_U, L0_ffn_lora_V)
    return x

_drawn_inputs = setup_inputs


def setup_inputs(seed=0):
    import zlib

    import numpy as np

    out = dict(_drawn_inputs(seed))
    spreads = {}
    factors = {'L0_ffn_gate_w': 4.328, 'L0_ffn_lora_U': 2.92, 'L0_ffn_lora_V': 2.934}
    for name, (base, spread) in spreads.items():
        noise = np.random.default_rng([zlib.crc32(name.encode()), seed]).standard_normal(out[name].shape)
        drawn = base * np.exp(spread * noise) if base else spread * noise
        out[name] = jnp.asarray(drawn.astype(out[name].dtype))
    for name, factor in factors.items():
        out[name] = (out[name] * factor).astype(out[name].dtype)
    return out
```

```python
from contextlib import ExitStack

import concourse.bass as bass
from concourse import mybir

F32 = mybir.dt.float32
F32R = mybir.dt.float32r
I32 = mybir.dt.int32
ALU = mybir.AluOpType
ACT = mybir.ActivationFunctionType
AX = mybir.AxisListType

P = 128
MASK_FILL = -99999.0
LN_EPS = 1e-5
DMA = 16


def flamingo_block(nc, x, ctx_t, mask, g_xattn, g_ffn, wq, wk, wv_t, ffn_t, lora_v, out):
    B, S, D = x.shape
    E, G = 8, 16
    ER = E * G
    C = D // P
    NT = S // P
    N_FFN = D + ER + E
    HALF = D // 2
    TILES = B * NT
    assert S == D == 512 and ER == P and ffn_t.shape[1] == N_FFN and lora_v.shape[0] == ER

    with ExitStack() as stack:
        def sb(name, shape, dt=F32):
            return stack.enter_context(nc.sbuf_tensor(name, shape, dt))

        def psum(name, shape):
            return stack.enter_context(nc.psum_tensor(name, shape, F32))

        def sem(name):
            return stack.enter_context(nc.semaphore(name))

        a_hl = sb("a_hl", [P, 2, C, D], F32R)
        wv_hl = sb("wv_hl", [P, 2, C, D], F32R)
        ffn_hl = sb("ffn_hl", [P, 2, C, N_FFN], F32R)
        lora_v_hl = sb("lora_v_hl", [P, 2, D], F32R)
        xn_t_hl = sb("xn_t_hl", [P, 2, C, S], F32R)
        q_t_hl = sb("q_t_hl", [P, 2, C, S], F32R)
        ctx_t_hl = sb("ctx_t_hl", [P, 2, C, S], F32R)
        v_hl = sb("v_hl", [P, 2, NT, D], F32R)
        p_t_hl = sb("p_t_hl", [P, 2, NT, P], F32R)
        x2_t_hl = sb("x2_t_hl", [P, 2, C, P], F32R)
        tg_t_hl = sb("tg_t_hl", [P, 2, P], F32R)
        wq_hl, wk_hl = v_hl, q_t_hl

        x_in = sb("x_in", [P, NT, D])
        x_res = sb("x_res", [P, NT, D])
        xn = sb("xn", [P, NT, D])
        ctx_raw = sb("ctx_raw", [P, C, S])
        mask_raw = sb("mask_raw", [P, S], I32)
        keep = sb("keep", [P, S])
        fill = sb("fill", [P, S])
        prob = sb("prob", [P, 2, S])
        x2 = sb("x2", [P, NT, D])
        x2n = sb("x2n", [P, 2, D])
        out_sb = sb("out_sb", [P, 2, D])
        stage = sb("stage", [P, C * D])
        stage_ffn = sb("stage_ffn", [P, C * (N_FFN - D) + D])
        wq_raw, wk_raw = x2, x_res
        ident = sb("ident", [P, P])
        minus_half = sb("minus_half", [P, 1])
        gains = sb("gains", [P, 2])
        tanh_g = sb("tanh_g", [P, 2])
        ln1_stats = sb("ln1_stats", [P, NT, 6])
        ln1_mv = sb("ln1_mv", [P, NT, 2])
        ln1_ve = sb("ln1_ve", [P, NT])
        ln1_rstd = sb("ln1_rstd", [P, NT])
        ln2_stats = sb("ln2_stats", [P, 6])
        ln2_mv = sb("ln2_mv", [P, 2, 2])
        ln2_ve = sb("ln2_ve", [P, 2])
        ln2_rstd = sb("ln2_rstd", [P, 2])
        neg_max = sb("neg_max", [P, 2])
        p_sum = sb("p_sum", [P, 2])
        p_inv = sb("p_inv", [P, 2])
        p_scale = sb("p_scale", [P, 2])
        gate_neg_max = sb("gate_neg_max", [P, 2])
        gate_exp = sb("gate_exp", [P, 2, E])
        gate_sum = sb("gate_sum", [P, 2])
        gate_inv = sb("gate_inv", [P, 2])
        tg = sb("tg", [P, 2, P])

        ps_score = psum("ps_score", [P, S])
        ps_ctx = psum("ps_ctx", [P, D])
        ps_work = [psum("ps_work0", [P, 512]), psum("ps_work1", [P, 512])]
        ps_ffn = [psum("ps_ffn0", [P, 2, 512]), psum("ps_ffn1", [P, 2, 512])]

        wq_in, wk_in, wv_in, ffn_in, lora_in, gain_in = map(sem, ("wq_in", "wk_in", "wv_in", "ffn_in", "lora_in", "gain_in"))
        x_loaded = [sem(f"x_loaded{j}") for j in range(NT)]
        ctx_loaded, mask_loaded = sem("ctx_loaded"), sem("mask_loaded")
        stored = [sem("stored0"), sem("stored1")]
        waits_passed = sem("waits_passed")
        ident_zeroed, consts_ready = sem("ident_zeroed"), sem("consts_ready")
        tanh_ready = sem("tanh_ready")
        weight_hi, weight_lo = sem("weight_hi"), sem("weight_lo")
        a_mm, a_hi, a_lo = sem("a_mm"), sem("a_hi"), sem("a_lo")
        v_mm, v_hi, v_lo = sem("v_mm"), sem("v_hi"), sem("v_lo")
        q_mm, q_hi, q_lo = sem("q_mm"), sem("q_hi"), sem("q_lo")
        xn_t_mm, xn_t_hi, xn_t_lo = sem("xn_t_mm"), sem("xn_t_hi"), sem("xn_t_lo")
        ln1_stat, ln1_aggr, xn_ready = sem("ln1_stat"), sem("ln1_aggr"), sem("xn_ready")
        x_kept = sem("x_kept")
        ln1_var, ln1_pow = sem("ln1_var"), sem("ln1_pow")
        ctx_hi, ctx_lo, mask_ready = sem("ctx_hi"), sem("ctx_lo"), sem("mask_ready")
        score_mm, score_masked, score_max, exp_done = sem("score_mm"), sem("score_masked"), sem("score_max"), sem("exp_done")
        p_t_mm, p_t_hi, p_t_lo = sem("p_t_mm"), sem("p_t_hi"), sem("p_t_lo")
        p_inverted, p_scaled = sem("p_inverted"), sem("p_scaled")
        ctx_mm, x2_ready = sem("ctx_mm"), sem("x2_ready")
        ln2_stat, ln2_aggr, ln2_var, ln2_pow, x2n_ready = (
            sem("ln2_stat"), sem("ln2_aggr"), sem("ln2_var"), sem("ln2_pow"), sem("x2n_ready"))
        x2_t_mm, x2_t_hi, x2_t_lo = sem("x2_t_mm"), sem("x2_t_hi"), sem("x2_t_lo")
        ffn_mm, gate_max, gate_exped, gate_inverted, tg_ready = (
            sem("ffn_mm"), sem("gate_max"), sem("gate_exped"), sem("gate_inverted"), sem("tg_ready"))
        tg_t_mm, tg_t_hi, tg_t_lo = sem("tg_t_mm"), sem("tg_t_hi"), sem("tg_t_lo")
        lora_mm, out_ready = sem("lora_mm"), sem("out_ready")

        def tile(b, i, back=0):
            b, i = b + (i - back) // NT, (i - back) % NT
            if isinstance(b, int) and not 0 <= b < B:
                return None
            return b, i

        def count(b, i):
            return b * NT + (i + 1)

        def halves(ap):
            return ap[:, 0], ap[:, 1]

        def f32(ap):
            return ap.bitcast(F32)

        def wait_apart(engine, semaphore, value):
            engine.wait_ge(semaphore, value)
            engine.sem_inc(waits_passed, 1)

        block = stack.enter_context(nc.Block())

        @block.sync
        def _(sp):
            def load_x(b, j):
                sp.dma_start(x_in[:, j, :], x[b, j * P:(j + 1) * P, :]).then_inc(x_loaded[j], DMA)

            def load_ctx(b):
                sp.dma_start(ctx_raw[:, :, :], ctx_t[b].rearrange("(c p) k -> p c k", p=P)).then_inc(ctx_loaded, DMA)

            def load_mask(b):
                sp.dma_start(mask_raw[:, :], mask.rearrange("(b o) s -> b o s", o=1)[b].broadcast_to([P, S])).then_inc(mask_loaded, DMA)

            def step(b, i):
                last = tile(b, i, 3)
                if last is not None:
                    sp.wait_ge(out_ready, count(*last))
                    lb, li = last
                    sp.dma_start(out[lb, li * P:(li + 1) * P, :], out_sb[:, li % 2, :]).then_inc(stored[li % 2], DMA)
                if i == 0 and tile(b, 0, -NT) is not None:
                    sp.wait_ge(ctx_lo, b + 1)
                    load_ctx(b + 1)
                    sp.wait_ge(mask_ready, 2 * (b + 1))
                    load_mask(b + 1)
                    for j in range(NT):
                        sp.wait_ge(x_kept, count(b, j))
                        sp.wait_ge(xn_ready, count(b, j))
                        load_x(b + 1, j)

            sp.dma_start(wk_raw[:, :, :], wk.rearrange("(c p) n -> p c n", p=P)).then_inc(wk_in, DMA)
            sp.dma_start(wq_raw[:, :, :], wq.rearrange("(c p) n -> p c n", p=P)).then_inc(wq_in, DMA)
            for j in range(NT):
                load_x(0, j)
            load_ctx(0)
            load_mask(0)
            sp.dma_start(stage[:, :].rearrange("p (c n) -> p c n", c=C), wv_t.rearrange("(c p) n -> p c n", p=P)).then_inc(wv_in, DMA)
            sp.dma_start(gains[:, 0:1], g_xattn.rearrange("(a n) -> a n", a=1).broadcast_to([P, 1])).then_inc(gain_in, DMA)
            sp.dma_start(gains[:, 1:2], g_ffn.rearrange("(a n) -> a n", a=1).broadcast_to([P, 1])).then_inc(gain_in, DMA)
            sp.dma_start(stage_ffn[:, 0:C * (N_FFN - D)].rearrange("p (c n) -> p c n", c=C),
                         ffn_t[:, D:].rearrange("(c p) n -> p c n", p=P)).then_inc(lora_in, DMA)
            sp.dma_start(stage_ffn[:, C * (N_FFN - D):], lora_v).then_inc(lora_in, DMA)
            sp.wait_ge(weight_lo, 3)
            sp.dma_start(stage[:, :].rearrange("p (c n) -> p c n", c=C),
                         ffn_t[:, 0:D].rearrange("(c p) n -> p c n", p=P)).then_inc(ffn_in, DMA)
            for i in range(NT):
                step(0, i)
            with sp.Fori(1, B - 1) as b:
                for i in range(NT):
                    step(b, i)
            for i in range(NT + 3):
                step(B - 1, i)
            for s in range(2):
                sp.wait_ge(stored[s], DMA * TILES // 2)

        @block.gpsimd
        def _(pool):
            def keep_x(b, j):
                if isinstance(b, int) and b == 0:
                    pool.wait_ge(x_loaded[j], DMA)
                else:
                    pool.wait_ge(x_loaded[j], (b + 1) * DMA)
                    wait_apart(pool, x2_ready, count(b - 1, j))
                nc.gpsimd.tensor_copy(x_res[:, j, :], x_in[:, j, :]).then_inc(x_kept, 1)

            def ln1_power(b):
                pool.wait_ge(ln1_var, b + 1)
                nc.gpsimd.tensor_tensor(ln1_rstd[:, :], ln1_ve[:, :], minus_half[:, :].broadcast_to([P, NT]), ALU.pow).then_inc(ln1_pow, 1)

            def step(b, i):
                t1 = tile(b, i, 1)
                if t1 is not None:
                    k = t1[1] % 2
                    pool.wait_ge(ln2_var, count(*t1))
                    nc.gpsimd.tensor_tensor(ln2_rstd[:, k:k + 1], ln2_ve[:, k:k + 1], minus_half[:, :], ALU.pow).then_inc(ln2_pow, 1)
                kept = tile(b, i, -(NT - 1))
                if kept is not None and not (isinstance(b, int) and b == 0 and i == 0):
                    keep_x(*kept)
                if i == 1 and tile(b, 0, -NT) is not None:
                    ln1_power(b + 1)

            nc.gpsimd.memset(ident[:, :], 0.0).then_inc(ident_zeroed, 1)
            nc.gpsimd.memset(minus_half[:, :], -0.5).then_inc(consts_ready, 1)
            pool.wait_ge(ident_zeroed, 1)
            nc.gpsimd.affine_select(out=ident[:, :], in_=ident[:, :], compare_op=ALU.not_equal, fill=1.0,
                                    base=0, pattern=[[-1, P]], channel_multiplier=1).then_inc(consts_ready, 1)
            pool.wait_ge(consts_ready, 2)
            ln1_power(0)
            pool.wait_ge(weight_lo, 1)
            for j in range(NT):
                keep_x(0, j)
            for i in range(NT):
                step(0, i)
            with pool.Fori(1, B - 1) as b:
                for i in range(NT):
                    step(b, i)
            for i in range(NT + 3):
                step(B - 1, i)

        @block.tensor
        def _(pe):
            def product(bank, lhs, rhs, cols, lhs_cols, k_chunks=C):
                for c in range(k_chunks):
                    for l, r in ((0, 0), (0, 1), (1, 0)):
                        mm = pe.matmul(bank, lhs[:, l, c, lhs_cols], rhs[:, r, c, cols],
                                       start=(c == 0 and l == r), stop=(c == k_chunks - 1 and l == 1))
                return mm

            def transposes(bank, tiles):
                for c, ap in enumerate(tiles):
                    mm = pe.transpose(bank[:, c * P:(c + 1) * P], ap, ident[:, :])
                return mm

            def step(b, i):
                t0, t1, t2, t3 = (tile(b, i, d) for d in range(4))
                if t1 is not None:
                    before = tile(b, i, 4)
                    if i == 0:
                        pe.wait_ge(q_lo, count(b, NT - 1))
                    elif i == 1:
                        pe.wait_ge(v_lo, count(b, NT - 1))
                    elif i == 3 and tile(b, 0, -NT) is not None:
                        pe.wait_ge(xn_t_lo, count(b + 1, NT - 1))
                    elif before is not None:
                        pe.wait_ge(tg_t_lo, count(*before))
                    pe.wait_ge(exp_done, count(*t1))
                    transposes(ps_work[0], [prob[:, t1[1] % 2, k * P:(k + 1) * P] for k in range(NT)]).then_inc(p_t_mm, 1)
                if t0 is not None:
                    if i == 0:
                        pe.wait_ge(q_lo, count(b, NT - 1))
                        pe.wait_ge(ctx_lo, b + 1)
                    if t1 is not None:
                        pe.wait_ge(score_masked, count(*t1))
                    product(ps_score[:, :], q_t_hl, ctx_t_hl, slice(0, S), slice(i * P, (i + 1) * P)).then_inc(score_mm, 1)
                if t2 is not None:
                    k = t2[1] % 2
                    pe.wait_ge(x2n_ready, count(*t2))
                    transposes(ps_work[1], [x2n[:, k, c * P:(c + 1) * P] for c in range(C)]).then_inc(x2_t_mm, 1)
                if t3 is not None:
                    k = t3[1] % 2
                    if t1 is not None:
                        pe.wait_ge(p_t_lo, count(*t1))
                    pe.wait_ge(tg_ready, count(*t3))
                    transposes(ps_work[0], [tg[:, k, :]]).then_inc(tg_t_mm, 1)
                if t1 is not None:
                    pe.wait_ge(p_t_lo, count(*t1))
                    if t1[1] == 0:
                        pe.wait_ge(v_lo, count(t1[0], NT - 1))
                    if t2 is not None:
                        pe.wait_ge(x2_ready, count(*t2))
                    product(ps_ctx[:, :], p_t_hl, v_hl, slice(0, D), slice(0, P)).then_inc(ctx_mm, 1)
                if t3 is not None:
                    pe.wait_ge(tg_t_lo, count(*t3))
                    bank = ps_ffn[t3[1] % 2]
                    for l, r in ((0, 0), (0, 1), (1, 0)):
                        for h in range(2):
                            mm = pe.matmul(bank[:, h, 0:HALF], tg_t_hl[:, l, :], lora_v_hl[:, r, h * HALF:(h + 1) * HALF],
                                           start=False, stop=(l == 1), skip_group_check=True)
                    mm.then_inc(lora_mm, 1)
                if t2 is not None:
                    pe.wait_ge(x2_t_lo, count(*t2))
                    if isinstance(t2[0], int) and t2 == (0, 0):
                        pe.wait_ge(weight_lo, 6)
                    t4 = tile(b, i, 4)
                    if t4 is not None:
                        pe.wait_ge(out_ready, count(*t4))
                    bank = ps_ffn[t2[1] % 2]
                    for c in range(C):
                        for l, r in ((0, 0), (0, 1), (1, 0)):
                            ends = dict(start=(c == 0 and l == r), stop=(c == C - 1 and l == 1))
                            pe.matmul(bank[:, 0, 0:HALF], x2_t_hl[:, l, c, :], ffn_hl[:, r, c, 0:HALF], **ends)
                            mm = pe.matmul(bank[:, 1, 0:N_FFN - HALF], x2_t_hl[:, l, c, :], ffn_hl[:, r, c, HALF:], **ends)
                    mm.then_inc(ffn_mm, 1)
                if i == 0:
                    values(b)
                if i == 2 and tile(b, 0, -NT) is not None:
                    for j in range(NT):
                        if j < 2:
                            if (t2, t3)[j] is not None:
                                pe.wait_ge((x2_t_lo, tg_t_lo)[j], count(*(t2, t3)[j]))
                        else:
                            pe.wait_ge(xn_t_lo, count(b + 1, j - 2))
                        xn_transposed(b + 1, j)
                if i == 3 and tile(b, 0, -NT) is not None:
                    pe.wait_ge(xn_t_lo, count(b + 1, NT - 1))
                    for c in range(C):
                        if c < 2:
                            if (t2, t3)[c] is not None:
                                pe.wait_ge((x2_t_lo, tg_t_lo)[c], count(*(t2, t3)[c]))
                        else:
                            pe.wait_ge(q_lo, count(b + 1, c - 2))
                        queries(c)

            def xn_transposed(b, j):
                pe.wait_ge(xn_ready, count(b, j))
                transposes(ps_work[(j + 1) % 2], [xn[:, j, c * P:(c + 1) * P] for c in range(C)]).then_inc(xn_t_mm, 1)

            def queries(c):
                product(ps_work[(c + 1) % 2][:, :], a_hl, xn_t_hl, slice(0, S), slice(c * P, (c + 1) * P)).then_inc(q_mm, 1)

            def values(b):
                t2, t3 = tile(b, 0, 2), tile(b, 0, 3)
                if isinstance(b, int) and b == 0:
                    pe.wait_ge(weight_lo, 3)
                for k in range(NT):
                    if k < 2:
                        if (t2, t3)[k] is not None:
                            pe.wait_ge((x2_t_lo, tg_t_lo)[k], count(*(t2, t3)[k]))
                    else:
                        pe.wait_ge(v_lo, count(b, k - 2))
                    product(ps_work[(k + 1) % 2][:, :], ctx_t_hl, wv_hl, slice(0, D), slice(k * P, (k + 1) * P)).then_inc(v_mm, 1)

            pe.wait_ge(weight_lo, 2)
            for c in range(C):
                if c >= 2:
                    pe.wait_ge(a_lo, c - 1)
                product(ps_work[(c + 1) % 2][:, :], wq_hl, wk_hl, slice(0, D), slice(c * P, (c + 1) * P)).then_inc(a_mm, 1)
            pe.wait_ge(consts_ready, 2)
            for j in range(NT):
                if j < 2:
                    pe.wait_ge(a_lo, j + 3)
                else:
                    pe.wait_ge(xn_t_lo, j - 1)
                xn_transposed(0, j)
            pe.wait_ge(xn_t_lo, NT)
            for c in range(C):
                if c >= 2:
                    pe.wait_ge(q_lo, c - 1)
                queries(c)
            for i in range(NT):
                step(0, i)
            with pe.Fori(1, B - 1) as b:
                for i in range(NT):
                    step(b, i)
            for i in range(NT + 3):
                step(B - 1, i)

        @block.scalar
        def _(act):
            def hi(ready, value, dst, src, done):
                act.wait_ge(ready, value)
                nc.scalar.activation(dst, src, ACT.Copy).then_inc(done, 1)

            def step(b, i):
                t0, t1, t2, t3 = (tile(b, i, d) for d in range(4))
                if t1 is not None:
                    hi(p_t_mm, count(*t1), p_t_hl[:, 0], ps_work[0][:, :], p_t_hi)
                if t2 is not None:
                    hi(x2_t_mm, count(*t2), x2_t_hl[:, 0], ps_work[1][:, :], x2_t_hi)
                if t3 is not None:
                    hi(tg_t_mm, count(*t3), tg_t_hl[:, 0], ps_work[0][:, 0:P], tg_t_hi)
                if t0 is not None:
                    k = i % 2
                    act.wait_ge(score_max, count(*t0))
                    nc.scalar.activation(prob[:, k, :], prob[:, k, :], ACT.Exp, bias=neg_max[:, k:k + 1], scale=-1.0,
                                         accum_out=p_sum[:, k:k + 1]).then_inc(exp_done, 1)
                if i == 3 and tile(b, 0, -NT) is not None:
                    act.wait_ge(score_mm, count(b, i))
                    hi(ctx_loaded, (b + 2) * DMA, ctx_t_hl[:, 0], ctx_raw[:, :, :], ctx_hi)
                if t2 is not None:
                    k = t2[1] % 2
                    act.wait_ge(gate_max, count(*t2))
                    nc.scalar.activation(gate_exp[:, k, :], ps_ffn[k][:, 1, N_FFN - HALF - E:N_FFN - HALF], ACT.Exp,
                                         bias=gate_neg_max[:, k:k + 1], accum_out=gate_sum[:, k:k + 1]).then_inc(gate_exped, 1)
                if i == 0:
                    for k in range(NT):
                        hi(v_mm, count(b, k), v_hl[:, 0, k, :], ps_work[(k + 1) % 2][:, :], v_hi)
                if i == 2 and tile(b, 0, -NT) is not None:
                    for j in range(NT):
                        xn_t_high(b + 1, j)
                if i == 3 and tile(b, 0, -NT) is not None:
                    for c in range(C):
                        q_high(b + 1, c)

            def xn_t_high(b, j):
                hi(xn_t_mm, count(b, j), xn_t_hl[:, 0, :, j * P:(j + 1) * P],
                   ps_work[(j + 1) % 2][:, :].rearrange("p (c n) -> p c n", c=C), xn_t_hi)

            def q_high(b, c):
                hi(q_mm, count(b, c), q_t_hl[:, 0, c, :], ps_work[(c + 1) % 2][:, :], q_hi)

            hi(wk_in, DMA, wk_hl[:, 0], wk_raw[:, :, :], weight_hi)
            hi(wq_in, DMA, wq_hl[:, 0], wq_raw[:, :, :], weight_hi)
            for c in range(C):
                hi(a_mm, c + 1, a_hl[:, 0, c, :], ps_work[(c + 1) % 2][:, :], a_hi)
            for j in range(NT):
                xn_t_high(0, j)
            hi(ctx_loaded, DMA, ctx_t_hl[:, 0], ctx_raw[:, :, :], ctx_hi)
            hi(wv_in, DMA, wv_hl[:, 0], stage[:, :].rearrange("p (c n) -> p c n", c=C), weight_hi)
            for c in range(C):
                q_high(0, c)
            act.wait_ge(gain_in, 2 * DMA)
            nc.scalar.activation(tanh_g[:, :], gains[:, :], ACT.Tanh).then_inc(tanh_ready, 1)
            hi(lora_in, 2 * DMA, ffn_hl[:, 0, :, D:], stage_ffn[:, 0:C * (N_FFN - D)].rearrange("p (c n) -> p c n", c=C), weight_hi)
            nc.scalar.activation(lora_v_hl[:, 0], stage_ffn[:, C * (N_FFN - D):], ACT.Copy, scale=1.0 / G).then_inc(weight_hi, 1)
            hi(ffn_in, DMA, ffn_hl[:, 0, :, 0:D], stage[:, :].rearrange("p (c n) -> p c n", c=C), weight_hi)
            for i in range(NT):
                step(0, i)
            with act.Fori(1, B - 1) as b:
                for i in range(NT):
                    step(b, i)
            for i in range(NT + 3):
                step(B - 1, i)

        @block.vector
        def _(dve):
            def lo(ready, value, dst, src, high, done):
                dve.wait_ge(ready, value)
                nc.vector.tensor_tensor(dst, src, f32(high), ALU.subtract).then_inc(done, 1)

            def make_mask(b):
                dve.wait_ge(mask_loaded, (b + 1) * DMA)
                nc.vector.tensor_scalar(keep[:, :], mask_raw[:, :], 0, None, ALU.not_equal).then_inc(mask_ready, 1)
                nc.vector.tensor_scalar(fill[:, :], mask_raw[:, :], 0, MASK_FILL, ALU.is_equal, ALU.mult).then_inc(mask_ready, 1)

            def ln1_statistics(b, j):
                dve.wait_ge(x_loaded[j], (b + 1) * DMA)
                nc.vector.bn_stats(ln1_stats[:, j, :], x_in[:, j, :]).then_inc(ln1_stat, 1)
                wait_apart(dve, ln1_stat, count(b, j))
                nc.vector.bn_aggr(ln1_mv[:, j, :], ln1_stats[:, j, :]).then_inc(ln1_aggr, 1)

            def ln1_variance(b):
                dve.wait_ge(ln1_aggr, count(b, NT - 1))
                nc.vector.tensor_scalar(ln1_ve[:, :], ln1_mv[:, :, 1], LN_EPS, None, ALU.add).then_inc(ln1_var, 1)

            def ln1_normalise(b):
                dve.wait_ge(ln1_pow, b + 1)
                for j in range(NT):
                    nc.vector.tensor_scalar(xn[:, j, :], x_in[:, j, :], ln1_mv[:, j, 0:1], ln1_rstd[:, j:j + 1],
                                            ALU.subtract, ALU.mult).then_inc(xn_ready, 1)

            def xn_t_low(b, j):
                lo(xn_t_hi, count(b, j), xn_t_hl[:, 1, :, j * P:(j + 1) * P],
                   ps_work[(j + 1) % 2][:, :].rearrange("p (c n) -> p c n", c=C), xn_t_hl[:, 0, :, j * P:(j + 1) * P], xn_t_lo)

            def q_low(b, c):
                lo(q_hi, count(b, c), q_t_hl[:, 1, c, :], ps_work[(c + 1) % 2][:, :], q_t_hl[:, 0, c, :], q_lo)

            def step(b, i):
                t0, t1, t2, t3 = (tile(b, i, d) for d in range(4))
                if t1 is not None:
                    lo(p_t_hi, count(*t1), p_t_hl[:, 1].rearrange("p k n -> p (k n)"), ps_work[0][:, :],
                       p_t_hl[:, 0].rearrange("p k n -> p (k n)"), p_t_lo)
                if t0 is not None:
                    k = i % 2
                    dve.wait_ge(score_mm, count(*t0))
                    if i == 0:
                        dve.wait_ge(mask_ready, 2 * (b + 1))
                    nc.vector.tensor_tensor(prob[:, k, :], ps_score[:, :], keep[:, :], ALU.mult).then_inc(score_masked, 1)
                    wait_apart(dve, score_masked, count(*t0))
                    nc.vector.tensor_tensor_reduce(prob[:, k, :], prob[:, k, :], fill[:, :], -1.0, 3.0e38, ALU.add, ALU.min,
                                                   neg_max[:, k:k + 1]).then_inc(score_max, 1)
                if t2 is not None:
                    lo(x2_t_hi, count(*t2), x2_t_hl[:, 1].rearrange("p k n -> p (k n)"), ps_work[1][:, :],
                       x2_t_hl[:, 0].rearrange("p k n -> p (k n)"), x2_t_lo)
                if t3 is not None:
                    lo(tg_t_hi, count(*t3), tg_t_hl[:, 1], ps_work[0][:, 0:P], tg_t_hl[:, 0], tg_t_lo)
                if t1 is not None:
                    b1, i1 = t1
                    k = i1 % 2
                    dve.wait_ge(exp_done, count(*t1))
                    nc.vector.reciprocal(p_inv[:, k:k + 1], p_sum[:, k:k + 1]).then_inc(p_inverted, 1)
                    if isinstance(b1, int) and t1 == (0, 0):
                        dve.wait_ge(tanh_ready, 1)
                    dve.wait_ge(p_inverted, count(*t1))
                    nc.vector.tensor_scalar(p_scale[:, k:k + 1], p_inv[:, k:k + 1], tanh_g[:, 0:1], None, ALU.mult).then_inc(p_scaled, 1)
                    dve.wait_ge(x_kept, count(*t1))
                    dve.wait_ge(p_scaled, count(*t1))
                    dve.wait_ge(ctx_mm, count(*t1))
                    nc.vector.scalar_tensor_tensor(x2[:, i1, :], ps_ctx[:, :], p_scale[:, k:k + 1], x_res[:, i1, :],
                                                   ALU.mult, ALU.add).then_inc(x2_ready, 1)
                    dve.wait_ge(x2_ready, count(*t1))
                    nc.vector.bn_stats(ln2_stats[:, :], x2[:, i1, :]).then_inc(ln2_stat, 1)
                    wait_apart(dve, ln2_stat, count(*t1))
                    nc.vector.bn_aggr(ln2_mv[:, k, :], ln2_stats[:, :]).then_inc(ln2_aggr, 1)
                    dve.wait_ge(ln2_aggr, count(*t1))
                    nc.vector.tensor_scalar(ln2_ve[:, k:k + 1], ln2_mv[:, k, 1:2], LN_EPS, None, ALU.add).then_inc(ln2_var, 1)
                if t3 is not None:
                    b3, i3 = t3
                    dve.wait_ge(lora_mm, count(*t3))
                    before = tile(b, i, 5)
                    if before is not None:
                        dve.wait_ge(stored[i3 % 2], DMA * (before[0] * (NT // 2) + (before[1] // 2 + 1)))
                    nc.vector.scalar_tensor_tensor(out_sb[:, i3 % 2, :].rearrange("p (h n) -> p h n", h=2),
                                                   ps_ffn[i3 % 2][:, :, 0:HALF], tanh_g[:, 1:2],
                                                   x2[:, i3, :].rearrange("p (h n) -> p h n", h=2),
                                                   ALU.mult, ALU.add).then_inc(out_ready, 1)
                if t1 is not None:
                    k = t1[1] % 2
                    dve.wait_ge(ln2_pow, count(*t1))
                    nc.vector.tensor_scalar(x2n[:, k, :], x2[:, t1[1], :], ln2_mv[:, k, 0:1], ln2_rstd[:, k:k + 1],
                                            ALU.subtract, ALU.mult).then_inc(x2n_ready, 1)
                if t2 is not None:
                    k = t2[1] % 2
                    n0 = N_FFN - HALF - E
                    dve.wait_ge(ffn_mm, count(*t2))
                    nc.vector.tensor_reduce(gate_neg_max[:, k:k + 1], ps_ffn[k][:, 1, n0:n0 + E], AX.X, ALU.max, negate=True).then_inc(gate_max, 1)
                    dve.wait_ge(gate_exped, count(*t2))
                    nc.vector.reciprocal(gate_inv[:, k:k + 1], gate_sum[:, k:k + 1]).then_inc(gate_inverted, 1)
                    dve.wait_ge(gate_inverted, count(*t2))
                    nc.vector.scalar_tensor_tensor(tg[:, k, :].rearrange("p (e r) -> p e r", e=E),
                                                   ps_ffn[k][:, 1, HALF:HALF + ER].rearrange("p (e r) -> p e r", e=E),
                                                   gate_inv[:, k:k + 1],
                                                   gate_exp[:, k, :].rearrange("p (e r) -> p e r", r=1).broadcast_to([P, E, G]),
                                                   ALU.mult, ALU.mult).then_inc(tg_ready, 1)
                more = tile(b, 0, -NT) is not None
                if i == 0:
                    for k in range(NT):
                        lo(v_hi, count(b, k), v_hl[:, 1, k, :], ps_work[(k + 1) % 2][:, :], v_hl[:, 0, k, :], v_lo)
                if i == 0 and more:
                    ln1_statistics(b + 1, 0)
                    ln1_statistics(b + 1, 1)
                if i == 1 and more:
                    ln1_statistics(b + 1, 2)
                    ln1_statistics(b + 1, 3)
                    ln1_variance(b + 1)
                    ln1_normalise(b + 1)
                if i == 2 and more:
                    for j in range(NT):
                        xn_t_low(b + 1, j)
                if i == 3 and more:
                    make_mask(b + 1)
                    lo(ctx_hi, b + 2, ctx_t_hl[:, 1], ctx_raw[:, :, :], ctx_t_hl[:, 0], ctx_lo)
                    for c in range(C):
                        q_low(b + 1, c)

            for j in range(NT):
                ln1_statistics(0, j)
            ln1_variance(0)
            ln1_normalise(0)
            lo(weight_hi, 1, wk_hl[:, 1], wk_raw[:, :, :], wk_hl[:, 0], weight_lo)
            lo(weight_hi, 2, wq_hl[:, 1], wq_raw[:, :, :], wq_hl[:, 0], weight_lo)
            for c in range(C):
                lo(a_hi, c + 1, a_hl[:, 1, c, :], ps_work[(c + 1) % 2][:, :], a_hl[:, 0, c, :], a_lo)
            for j in range(NT):
                xn_t_low(0, j)
            make_mask(0)
            lo(ctx_hi, 1, ctx_t_hl[:, 1], ctx_raw[:, :, :], ctx_t_hl[:, 0], ctx_lo)
            lo(weight_hi, 3, wv_hl[:, 1], stage[:, :].rearrange("p (c n) -> p c n", c=C), wv_hl[:, 0], weight_lo)
            for c in range(C):
                q_low(0, c)
            lo(weight_hi, 4, ffn_hl[:, 1, :, D:], stage_ffn[:, 0:C * (N_FFN - D)].rearrange("p (c n) -> p c n", c=C),
               ffn_hl[:, 0, :, D:], weight_lo)
            dve.wait_ge(weight_hi, 5)
            nc.vector.scalar_tensor_tensor(lora_v_hl[:, 1], stage_ffn[:, C * (N_FFN - D):], 1.0 / G, f32(lora_v_hl[:, 0]),
                                           ALU.mult, ALU.subtract).then_inc(weight_lo, 1)
            lo(weight_hi, 6, ffn_hl[:, 1, :, 0:D], stage[:, :].rearrange("p (c n) -> p c n", c=C), ffn_hl[:, 0, :, 0:D], weight_lo)
            for i in range(NT):
                step(0, i)
            with dve.Fori(1, B - 1) as b:
                for i in range(NT):
                    step(b, i)
            for i in range(NT + 3):
                step(B - 1, i)


def kernel(x, ctx_1024, mask_BxS2_ik1, g_xattn, g_ffn, L0_xattn_Wq, L0_xattn_Wk, L0_xattn_Wv,
           L0_ffn_weight, L0_ffn_gate_w, L0_ffn_lora_U, L0_ffn_lora_V):
    import numpy as np
    import concourse.bacc as bacc
    from concourse.bass_utils import run_bass_kernel_spmd

    arr = lambda a: np.ascontiguousarray(np.asarray(a))
    E, R, D = L0_ffn_lora_U.shape
    arrays = {
        "x": arr(x),
        "ctx_t": arr(np.asarray(ctx_1024).transpose(0, 2, 1)),
        "mask": arr(mask_BxS2_ik1),
        "g_xattn": arr(g_xattn),
        "g_ffn": arr(g_ffn),
        "wq": arr(L0_xattn_Wq),
        "wk": arr(L0_xattn_Wk),
        "wv_t": arr(np.asarray(L0_xattn_Wv).T),
        "ffn_t": arr(np.concatenate([np.asarray(L0_ffn_weight), np.asarray(L0_ffn_lora_U).reshape(E * R, D),
                                     np.asarray(L0_ffn_gate_w)]).T),
        "lora_v": arr(np.asarray(L0_ffn_lora_V).transpose(0, 2, 1).reshape(E * R, -1)),
    }
    nc = bacc.Bacc("TRN2", target_bir_lowering=False, num_devices=1)
    args = [nc.dram_tensor(f"in_{n}", a.shape, mybir.dt.from_np(a.dtype), kind="ExternalInput").ap() for n, a in arrays.items()]
    out = nc.dram_tensor("out", arrays["x"].shape, F32, kind="ExternalOutput").ap()
    flamingo_block(nc, *args, out)
    r = run_bass_kernel_spmd(nc, [{f"in_{n}": a for n, a in arrays.items()}], core_ids=[0])
    return r.results[0]["out"]
```

```python
from contextlib import ExitStack

import concourse.bass as bass
from concourse import mybir

F32 = mybir.dt.float32
F32R = mybir.dt.float32r
I32 = mybir.dt.int32
ALU = mybir.AluOpType
ACT = mybir.ActivationFunctionType
AX = mybir.AxisListType

P = 128
MASK_FILL = -99999.0
LN_EPS = 1e-5
DMA = 16


def flamingo_block(nc, x, x_t, ctx_t, mask, g_xattn, g_ffn, wq, wk, wv_t, ffn_t, lora_v, out):
    B, S, D = x.shape
    E, G = 8, 16
    ER = E * G
    C = D // P
    NT = S // P
    N_FFN = D + ER + E
    HALF = D // 2
    TILES = B * NT
    assert S == D == 512 and ER == P and ffn_t.shape[1] == N_FFN and lora_v.shape[0] == ER

    with ExitStack() as stack:
        def sb(name, shape, dt=F32):
            return stack.enter_context(nc.sbuf_tensor(name, shape, dt))

        def psum(name, shape):
            return stack.enter_context(nc.psum_tensor(name, shape, F32))

        def sem(name):
            return stack.enter_context(nc.semaphore(name))

        a_hl = sb("a_hl", [P, 2, C, D], F32R)
        wv_hl = sb("wv_hl", [P, 2, C, D], F32R)
        ffn_hl = sb("ffn_hl", [P, 2, C, N_FFN], F32R)
        lora_v_hl = sb("lora_v_hl", [P, 2, D], F32R)
        x_t_hl = sb("x_t_hl", [P, 2, C, S], F32R)
        q_t_hl = sb("q_t_hl", [P, 2, C, S], F32R)
        ctx_t_hl = sb("ctx_t_hl", [P, 2, C, S], F32R)
        v_hl = sb("v_hl", [P, 2, NT, D], F32R)
        p_t_hl = sb("p_t_hl", [P, 2, NT, P], F32R)
        x2_t_hl = sb("x2_t_hl", [P, 2, C, P], F32R)
        tg_t_hl = sb("tg_t_hl", [P, 2, P], F32R)
        wq_hl, wk_hl = v_hl, q_t_hl

        x_in = sb("x_in", [P, NT, D])
        x_res = sb("x_res", [P, NT, D])
        x_t_raw = sb("x_t_raw", [P, C, S])
        ctx_raw = sb("ctx_raw", [P, C, S])
        mask_raw = sb("mask_raw", [P, S], I32)
        keep = sb("keep", [P, S])
        fill = sb("fill", [P, S])
        prob = sb("prob", [P, 2, S])
        x2 = sb("x2", [P, NT, D])
        x2n = sb("x2n", [P, 2, D])
        out_sb = sb("out_sb", [P, 2, D])
        stage = sb("stage", [P, C * D])
        stage_ffn = sb("stage_ffn", [P, C * (N_FFN - D) + D])
        wq_raw, wk_raw = x2, x_res
        wq_sum = sb("wq_sum", [P, C])
        wq_neg_mean = sb("wq_neg_mean", [P, C])
        ident = sb("ident", [P, P])
        minus_half = sb("minus_half", [P, 1])
        gains = sb("gains", [P, 2])
        tanh_g = sb("tanh_g", [P, 2])
        ln1_stats = sb("ln1_stats", [P, NT, 6])
        ln1_mv = sb("ln1_mv", [P, NT, 2])
        ln1_ve = sb("ln1_ve", [P, NT])
        ln1_rstd = sb("ln1_rstd", [P, NT])
        ln2_stats = sb("ln2_stats", [P, 6])
        ln2_mv = sb("ln2_mv", [P, 2, 2])
        ln2_ve = sb("ln2_ve", [P, 2])
        ln2_rstd = sb("ln2_rstd", [P, 2])
        neg_max = sb("neg_max", [P, 2])
        p_sum = sb("p_sum", [P, 2])
        p_inv = sb("p_inv", [P, 2])
        p_scale = sb("p_scale", [P, 2])
        gate_neg_max = sb("gate_neg_max", [P, 2])
        gate_exp = sb("gate_exp", [P, 2, E])
        gate_sum = sb("gate_sum", [P, 2])
        gate_inv = sb("gate_inv", [P, 2])
        tg = sb("tg", [P, 2, P])

        ps_score = psum("ps_score", [P, S])
        ps_ctx = psum("ps_ctx", [P, D])
        ps_work = [psum("ps_work0", [P, 512]), psum("ps_work1", [P, 512])]
        ps_ffn = [psum("ps_ffn0", [P, 2, 512]), psum("ps_ffn1", [P, 2, 512])]

        wqk_in = [sem(f"wqk_in{c}") for c in range(C)]
        wv_in, ffn_in, lora_in, gain_in = map(sem, ("wv_in", "ffn_in", "lora_in", "gain_in"))
        x_loaded = [sem(f"x_loaded{j}") for j in range(NT)]
        x_t_loaded, ctx_loaded, mask_loaded = sem("x_t_loaded"), sem("ctx_loaded"), sem("mask_loaded")
        stored = [sem("stored0"), sem("stored1")]
        waits_passed = sem("waits_passed")
        ident_zeroed, consts_ready = sem("ident_zeroed"), sem("consts_ready")
        tanh_ready = sem("tanh_ready")
        wq_summed, wq_mean, wk_hi, wq_hi, wqk_lo = map(sem, ("wq_summed", "wq_mean", "wk_hi", "wq_hi", "wqk_lo"))
        weight_hi, weight_lo = sem("weight_hi"), sem("weight_lo")
        a_mm, a_hi, a_lo = sem("a_mm"), sem("a_hi"), sem("a_lo")
        v_mm, v_hi, v_lo = sem("v_mm"), sem("v_hi"), sem("v_lo")
        q_mm, q_hi, q_lo = sem("q_mm"), sem("q_hi"), sem("q_lo")
        x_t_hi, x_t_lo = sem("x_t_hi"), sem("x_t_lo")
        ln1_stat, ln1_aggr = sem("ln1_stat"), sem("ln1_aggr")
        x_kept = sem("x_kept")
        ln1_var, ln1_pow = sem("ln1_var"), sem("ln1_pow")
        ctx_hi, ctx_lo, mask_ready = sem("ctx_hi"), sem("ctx_lo"), sem("mask_ready")
        score_mm, score_masked, score_max, exp_done = sem("score_mm"), sem("score_masked"), sem("score_max"), sem("exp_done")
        p_t_mm, p_t_hi, p_t_lo = sem("p_t_mm"), sem("p_t_hi"), sem("p_t_lo")
        p_inverted, p_scaled = sem("p_inverted"), sem("p_scaled")
        ctx_mm, x2_ready = sem("ctx_mm"), sem("x2_ready")
        ln2_stat, ln2_aggr, ln2_var, ln2_pow, x2n_ready = (
            sem("ln2_stat"), sem("ln2_aggr"), sem("ln2_var"), sem("ln2_pow"), sem("x2n_ready"))
        x2_t_mm, x2_t_hi, x2_t_lo = sem("x2_t_mm"), sem("x2_t_hi"), sem("x2_t_lo")
        ffn_mm, gate_max, gate_exped, gate_inverted, tg_ready = (
            sem("ffn_mm"), sem("gate_max"), sem("gate_exped"), sem("gate_inverted"), sem("tg_ready"))
        tg_t_mm, tg_t_hi, tg_t_lo = sem("tg_t_mm"), sem("tg_t_hi"), sem("tg_t_lo")
        lora_mm, out_ready = sem("lora_mm"), sem("out_ready")

        def tile(b, i, back=0):
            b, i = b + (i - back) // NT, (i - back) % NT
            if isinstance(b, int) and not 0 <= b < B:
                return None
            return b, i

        def count(b, i):
            return b * NT + (i + 1)

        WORK = (0, 1, 0, 1)

        def p_t_bank(step):
            return ps_work[WORK[step % NT]]

        def x2_t_bank(step):
            return ps_work[1 - WORK[step % NT]]

        def v_bank(k):
            return ps_work[(k + 1) % 2]

        def q_bank(c):
            return ps_work[c % 2]

        def a_bank(m):
            return ps_ffn[m // 2][:, m % 2, :]

        def values_of(b):
            return (2, 3) if isinstance(b, int) and b == 0 else (0, 1, 2, 3)

        def pieces_of(i):
            return {1: (0, 1), 2: (2, 3)}[i]

        def f32(ap):
            return ap.bitcast(F32)

        def wait_apart(engine, semaphore, value):
            engine.wait_ge(semaphore, value)
            engine.sem_inc(waits_passed, 1)

        block = stack.enter_context(nc.Block())

        @block.sync
        def _(sp):
            def load_x(b, j):
                sp.dma_start(x_in[:, j, :], x[b, j * P:(j + 1) * P, :]).then_inc(x_loaded[j], DMA)

            def load_x_t(b):
                sp.dma_start(x_t_raw[:, :, :], x_t[b].rearrange("(c p) n -> p c n", p=P)).then_inc(x_t_loaded, DMA)

            def load_ctx(b):
                sp.dma_start(ctx_raw[:, :, :], ctx_t[b].rearrange("(c p) k -> p c k", p=P)).then_inc(ctx_loaded, DMA)

            def load_mask(b):
                sp.dma_start(mask_raw[:, :], mask.rearrange("(b o) s -> b o s", o=1)[b].broadcast_to([P, S])).then_inc(mask_loaded, DMA)

            def step(b, i):
                last = tile(b, i, 3)
                if last is not None:
                    sp.wait_ge(out_ready, count(*last))
                    lb, li = last
                    sp.dma_start(out[lb, li * P:(li + 1) * P, :], out_sb[:, li % 2, :]).then_inc(stored[li % 2], DMA)
                if i == 0 and tile(b, 0, -NT) is not None:
                    sp.wait_ge(x_t_lo, count(b, NT - 1))
                    load_x_t(b + 1)
                    sp.wait_ge(ctx_lo, b + 1)
                    load_ctx(b + 1)
                    sp.wait_ge(mask_ready, 2 * (b + 1))
                    load_mask(b + 1)
                    for j in range(NT):
                        sp.wait_ge(x_kept, count(b, j))
                        sp.wait_ge(ln1_stat, count(b, j))
                        load_x(b + 1, j)

            for c in range(C):
                for raw, w in ((wq_raw, wq), (wk_raw, wk)):
                    sp.dma_start(raw[:, c, :], w[c * P:(c + 1) * P, :]).then_inc(wqk_in[c], DMA)
            load_ctx(0)
            sp.dma_start(stage[:, :].rearrange("p (c n) -> p c n", c=C), wv_t.rearrange("(c p) n -> p c n", p=P)).then_inc(wv_in, DMA)
            load_x_t(0)
            load_mask(0)
            for j in range(NT):
                load_x(0, j)
            sp.dma_start(gains[:, 0:1], g_xattn.rearrange("(a n) -> a n", a=1).broadcast_to([P, 1])).then_inc(gain_in, DMA)
            sp.dma_start(gains[:, 1:2], g_ffn.rearrange("(a n) -> a n", a=1).broadcast_to([P, 1])).then_inc(gain_in, DMA)
            sp.dma_start(stage_ffn[:, 0:C * (N_FFN - D)].rearrange("p (c n) -> p c n", c=C),
                         ffn_t[:, D:].rearrange("(c p) n -> p c n", p=P)).then_inc(lora_in, DMA)
            sp.dma_start(stage_ffn[:, C * (N_FFN - D):], lora_v).then_inc(lora_in, DMA)
            sp.wait_ge(weight_lo, 1)
            sp.dma_start(stage[:, :].rearrange("p (c n) -> p c n", c=C),
                         ffn_t[:, 0:D].rearrange("(c p) n -> p c n", p=P)).then_inc(ffn_in, DMA)
            for i in range(NT):
                step(0, i)
            with sp.Fori(1, B - 1) as b:
                for i in range(NT):
                    step(b, i)
            for i in range(NT + 3):
                step(B - 1, i)
            for s in range(2):
                sp.wait_ge(stored[s], DMA * TILES // 2)

        @block.gpsimd
        def _(pool):
            def keep_x(b, j):
                if isinstance(b, int) and b == 0:
                    pool.wait_ge(x_loaded[j], DMA)
                else:
                    pool.wait_ge(x_loaded[j], (b + 1) * DMA)
                    wait_apart(pool, x2_ready, count(b - 1, j))
                nc.gpsimd.tensor_copy(x_res[:, j, :], x_in[:, j, :]).then_inc(x_kept, 1)

            def ln1_power(b):
                pool.wait_ge(ln1_var, b + 1)
                if not (isinstance(b, int) and b == 0):
                    pool.wait_ge(score_masked, count(b - 1, NT - 1))
                nc.gpsimd.tensor_tensor(ln1_rstd[:, :], ln1_ve[:, :], minus_half[:, :].broadcast_to([P, NT]), ALU.pow).then_inc(ln1_pow, 1)

            def step(b, i):
                t1 = tile(b, i, 1)
                if t1 is not None:
                    k = t1[1] % 2
                    pool.wait_ge(ln2_var, count(*t1))
                    nc.gpsimd.tensor_tensor(ln2_rstd[:, k:k + 1], ln2_ve[:, k:k + 1], minus_half[:, :], ALU.pow).then_inc(ln2_pow, 1)
                kept = tile(b, i, -(NT - 1))
                if kept is not None and not (isinstance(b, int) and b == 0 and i == 0):
                    keep_x(*kept)
                if i == 3 and tile(b, 0, -NT) is not None:
                    ln1_power(b + 1)

            nc.gpsimd.memset(ident[:, :], 0.0).then_inc(ident_zeroed, 1)
            nc.gpsimd.memset(minus_half[:, :], -0.5).then_inc(consts_ready, 1)
            pool.wait_ge(ident_zeroed, 1)
            nc.gpsimd.affine_select(out=ident[:, :], in_=ident[:, :], compare_op=ALU.not_equal, fill=1.0,
                                    base=0, pattern=[[-1, P]], channel_multiplier=1).then_inc(consts_ready, 1)
            pool.wait_ge(consts_ready, 2)
            ln1_power(0)
            pool.wait_ge(wqk_lo, 2 * C)
            for j in range(NT):
                keep_x(0, j)
            for i in range(NT):
                step(0, i)
            with pool.Fori(1, B - 1) as b:
                for i in range(NT):
                    step(b, i)
            for i in range(NT + 3):
                step(B - 1, i)

        @block.tensor
        def _(pe):
            def product(bank, lhs, rhs, cols, lhs_cols, k_chunks=C, chunk_wait=None):
                for c in range(k_chunks):
                    if chunk_wait:
                        chunk_wait(c)
                    for l, r in ((0, 0), (0, 1), (1, 0)):
                        mm = pe.matmul(bank, lhs[:, l, c, lhs_cols], rhs[:, r, c, cols],
                                       start=(c == 0 and l == r), stop=(c == k_chunks - 1 and l == 1))
                return mm

            def transposes(bank, tiles):
                for c, ap in enumerate(tiles):
                    mm = pe.transpose(bank[:, c * P:(c + 1) * P], ap, ident[:, :])
                return mm

            def step(b, i):
                t0, t1, t2, t3 = (tile(b, i, d) for d in range(4))
                more = tile(b, 0, -NT) is not None
                if i == 0:
                    before = (q_lo, count(b, 2)), (q_lo, count(b, 3))
                elif i == 1:
                    before = (v_lo, count(b, 2)), (v_lo, count(b, 3))
                else:
                    before = (x2_t_lo, tile(b, i, 3)), (tg_t_lo, tile(b, i, 4))
                    before = [(s, count(*t)) if t is not None else None for s, t in before]
                if t1 is not None:
                    if before[0]:
                        pe.wait_ge(*before[0])
                    if isinstance(t1[0], int) and t1 == (0, 0):
                        pe.wait_ge(consts_ready, 2)
                    pe.wait_ge(exp_done, count(*t1))
                    transposes(p_t_bank(i), [prob[:, t1[1] % 2, k * P:(k + 1) * P] for k in range(NT)]).then_inc(p_t_mm, 1)
                if t0 is not None:
                    if i == 0:
                        pe.wait_ge(ctx_lo, b + 1)
                    if t1 is not None:
                        pe.wait_ge(score_masked, count(*t1))
                    product(ps_score[:, :], q_t_hl, ctx_t_hl, slice(0, S), slice(i * P, (i + 1) * P),
                            chunk_wait=(lambda c: pe.wait_ge(q_lo, count(b, c))) if i == 0 else None).then_inc(score_mm, 1)
                if t2 is not None:
                    k = t2[1] % 2
                    if before[1]:
                        pe.wait_ge(*before[1])
                    pe.wait_ge(x2n_ready, count(*t2))
                    transposes(x2_t_bank(i), [x2n[:, k, c * P:(c + 1) * P] for c in range(C)]).then_inc(x2_t_mm, 1)
                if t3 is not None:
                    k = t3[1] % 2
                    if t1 is not None:
                        pe.wait_ge(p_t_lo, count(*t1))
                    pe.wait_ge(tg_ready, count(*t3))
                    transposes(p_t_bank(i), [tg[:, k, :]]).then_inc(tg_t_mm, 1)
                if t1 is not None:
                    pe.wait_ge(p_t_lo, count(*t1))
                    if t1[1] == 0:
                        pe.wait_ge(v_lo, count(t1[0], NT - 1))
                    if t2 is not None:
                        pe.wait_ge(x2_ready, count(*t2))
                    product(ps_ctx[:, :], p_t_hl, v_hl, slice(0, D), slice(0, P)).then_inc(ctx_mm, 1)
                if t3 is not None:
                    pe.wait_ge(tg_t_lo, count(*t3))
                    bank = ps_ffn[t3[1] % 2]
                    for l, r in ((0, 0), (0, 1), (1, 0)):
                        for h in range(2):
                            mm = pe.matmul(bank[:, h, 0:HALF], tg_t_hl[:, l, :], lora_v_hl[:, r, h * HALF:(h + 1) * HALF],
                                           start=False, stop=(l == 1), skip_group_check=True)
                    mm.then_inc(lora_mm, 1)
                if t2 is not None:
                    pe.wait_ge(x2_t_lo, count(*t2))
                    if isinstance(t2[0], int) and t2 == (0, 0):
                        pe.wait_ge(weight_lo, 4)
                    t4 = tile(b, i, 4)
                    if t4 is not None:
                        pe.wait_ge(out_ready, count(*t4))
                    for h, cols in ((1, slice(HALF, N_FFN)), (0, slice(0, HALF))):
                        bank = ps_ffn[t2[1] % 2][:, h, 0:cols.stop - cols.start]
                        mm = product(bank, x2_t_hl, ffn_hl, cols, slice(0, P))
                        if h == 1:
                            mm.then_inc(ffn_mm, 1)
                if i == 0:
                    for k in values_of(b):
                        if k >= 2:
                            pe.wait_ge(v_lo, count(b, k - 2))
                        elif (t2, t3)[k] is not None:
                            pe.wait_ge((x2_t_lo, tg_t_lo)[k], count(*(t2, t3)[k]))
                        values(k)
                if i == 3 and more:
                    pe.wait_ge(x_t_lo, count(b + 1, NT - 1))
                    for c in range(C):
                        if c >= 2:
                            pe.wait_ge(q_lo, count(b + 1, c - 2))
                        elif (t2, t3)[c] is not None:
                            pe.wait_ge((x2_t_lo, tg_t_lo)[c], count(*(t2, t3)[c]))
                        queries(c)

            def queries(c):
                product(q_bank(c)[:, :], a_hl, x_t_hl, slice(0, S), slice(c * P, (c + 1) * P)).then_inc(q_mm, 1)

            def values(k):
                product(v_bank(k)[:, :], ctx_t_hl, wv_hl, slice(0, D), slice(k * P, (k + 1) * P)).then_inc(v_mm, 1)

            for c in range(C):
                pe.wait_ge(wqk_lo, 2 * (c + 1))
                for m in range(C):
                    for l, r in ((0, 0), (0, 1), (1, 0)):
                        mm = pe.matmul(a_bank(m), wq_hl[:, l, c, m * P:(m + 1) * P], wk_hl[:, r, c, :],
                                       start=(c == 0 and l == r), stop=(c == C - 1 and l == 1))
                    if c == C - 1:
                        mm.then_inc(a_mm, 1)
            pe.wait_ge(ctx_lo, 1)
            pe.wait_ge(weight_lo, 1)
            values(0)
            values(1)
            pe.wait_ge(a_lo, C)
            pe.wait_ge(x_t_lo, NT)
            for c in range(C):
                if c < 2:
                    pe.wait_ge(v_lo, 2 - c)
                else:
                    pe.wait_ge(q_lo, c - 1)
                queries(c)
            for i in range(NT):
                step(0, i)
            with pe.Fori(1, B - 1) as b:
                for i in range(NT):
                    step(b, i)
            for i in range(NT + 3):
                step(B - 1, i)

        @block.scalar
        def _(act):
            def hi(ready, value, dst, src, done):
                act.wait_ge(ready, value)
                nc.scalar.activation(dst, src, ACT.Copy).then_inc(done, 1)

            def step(b, i):
                t0, t1, t2, t3 = (tile(b, i, d) for d in range(4))
                more = tile(b, 0, -NT) is not None
                if t1 is not None:
                    hi(p_t_mm, count(*t1), p_t_hl[:, 0], p_t_bank(i)[:, :], p_t_hi)
                if t2 is not None:
                    hi(x2_t_mm, count(*t2), x2_t_hl[:, 0], x2_t_bank(i)[:, :], x2_t_hi)
                if t3 is not None:
                    hi(tg_t_mm, count(*t3), tg_t_hl[:, 0], p_t_bank(i)[:, 0:P], tg_t_hi)
                if t0 is not None:
                    k = i % 2
                    act.wait_ge(score_max, count(*t0))
                    nc.scalar.activation(prob[:, k, :], prob[:, k, :], ACT.Exp, bias=neg_max[:, k:k + 1], scale=-1.0,
                                         accum_out=p_sum[:, k:k + 1]).then_inc(exp_done, 1)
                if i == 3 and more:
                    act.wait_ge(score_mm, count(b, i))
                    hi(ctx_loaded, (b + 2) * DMA, ctx_t_hl[:, 0], ctx_raw[:, :, :], ctx_hi)
                if i in (1, 2) and more:
                    for c in pieces_of(i):
                        x_t_high(b + 1, c)
                if t2 is not None:
                    k = t2[1] % 2
                    act.wait_ge(gate_max, count(*t2))
                    nc.scalar.activation(gate_exp[:, k, :], ps_ffn[k][:, 1, N_FFN - HALF - E:N_FFN - HALF], ACT.Exp,
                                         bias=gate_neg_max[:, k:k + 1], accum_out=gate_sum[:, k:k + 1]).then_inc(gate_exped, 1)
                if i == 0:
                    for k in values_of(b):
                        v_high(b, k)
                if i == 3 and more:
                    for c in range(C):
                        q_high(b + 1, c)

            def v_high(b, k):
                hi(v_mm, count(b, k), v_hl[:, 0, k, :], v_bank(k)[:, :], v_hi)

            def x_t_high(b, c):
                if c == 0 and not (isinstance(b, int) and b == 0):
                    act.wait_ge(q_mm, count(b - 1, C - 1))
                hi(x_t_loaded, (b + 1) * DMA, x_t_hl[:, 0, c, :], x_t_raw[:, c, :], x_t_hi)

            def q_high(b, c):
                hi(q_mm, count(b, c), q_t_hl[:, 0, c, :], q_bank(c)[:, :], q_hi)

            for c in range(C):
                act.wait_ge(wqk_in[c], 2 * DMA)
                nc.scalar.activation(out_sb[:, c % 2, :], wq_raw[:, c, :], ACT.Copy, accum_out=wq_sum[:, c:c + 1]).then_inc(wq_summed, 1)
                nc.scalar.activation(wk_hl[:, 0, c, :], wk_raw[:, c, :], ACT.Copy).then_inc(wk_hi, 1)
                act.wait_ge(wq_mean, c + 1)
                nc.scalar.activation(wq_hl[:, 0, c, :], wq_raw[:, c, :], ACT.Identity, bias=wq_neg_mean[:, c:c + 1]).then_inc(wq_hi, 1)
            hi(ctx_loaded, DMA, ctx_t_hl[:, 0], ctx_raw[:, :, :], ctx_hi)
            hi(wv_in, DMA, wv_hl[:, 0], stage[:, :].rearrange("p (c n) -> p c n", c=C), weight_hi)
            for c in range(C):
                x_t_high(0, c)
            for m in range(C):
                hi(a_mm, m + 1, a_hl[:, 0, m, :], a_bank(m), a_hi)
            v_high(0, 0)
            v_high(0, 1)
            act.wait_ge(gain_in, 2 * DMA)
            nc.scalar.activation(tanh_g[:, :], gains[:, :], ACT.Tanh).then_inc(tanh_ready, 1)
            hi(lora_in, 2 * DMA, ffn_hl[:, 0, :, D:], stage_ffn[:, 0:C * (N_FFN - D)].rearrange("p (c n) -> p c n", c=C), weight_hi)
            nc.scalar.activation(lora_v_hl[:, 0], stage_ffn[:, C * (N_FFN - D):], ACT.Copy, scale=1.0 / G).then_inc(weight_hi, 1)
            hi(ffn_in, DMA, ffn_hl[:, 0, :, 0:D], stage[:, :].rearrange("p (c n) -> p c n", c=C), weight_hi)
            for c in range(C):
                q_high(0, c)
            for i in range(NT):
                step(0, i)
            with act.Fori(1, B - 1) as b:
                for i in range(NT):
                    step(b, i)
            for i in range(NT + 3):
                step(B - 1, i)

        @block.vector
        def _(dve):
            def lo(ready, value, dst, src, high, done):
                dve.wait_ge(ready, value)
                nc.vector.tensor_tensor(dst, src, f32(high), ALU.subtract).then_inc(done, 1)

            def make_mask(b):
                dve.wait_ge(mask_loaded, (b + 1) * DMA)
                nc.vector.tensor_scalar(keep[:, :], mask_raw[:, :], 0, None, ALU.not_equal).then_inc(mask_ready, 1)
                nc.vector.tensor_scalar(fill[:, :], mask_raw[:, :], 0, MASK_FILL, ALU.is_equal, ALU.mult).then_inc(mask_ready, 1)

            def ln1_statistics(b, j):
                dve.wait_ge(x_loaded[j], (b + 1) * DMA)
                nc.vector.bn_stats(ln1_stats[:, j, :], x_in[:, j, :]).then_inc(ln1_stat, 1)
                wait_apart(dve, ln1_stat, count(b, j))
                nc.vector.bn_aggr(ln1_mv[:, j, :], ln1_stats[:, j, :]).then_inc(ln1_aggr, 1)

            def ln1_variance(b):
                dve.wait_ge(ln1_aggr, count(b, NT - 1))
                nc.vector.tensor_scalar(ln1_ve[:, :], ln1_mv[:, :, 1], LN_EPS, None, ALU.add).then_inc(ln1_var, 1)

            def x_t_low(b, c):
                lo(x_t_hi, count(b, c), x_t_hl[:, 1, c, :], x_t_raw[:, c, :], x_t_hl[:, 0, c, :], x_t_lo)

            def v_low(b, k):
                lo(v_hi, count(b, k), v_hl[:, 1, k, :], v_bank(k)[:, :], v_hl[:, 0, k, :], v_lo)

            def q_low(b, c):
                lo(q_hi, count(b, c), q_t_hl[:, 1, c, :], q_bank(c)[:, :], q_t_hl[:, 0, c, :], q_lo)

            def step(b, i):
                t0, t1, t2, t3 = (tile(b, i, d) for d in range(4))
                if t1 is not None:
                    lo(p_t_hi, count(*t1), p_t_hl[:, 1].rearrange("p k n -> p (k n)"), p_t_bank(i)[:, :],
                       p_t_hl[:, 0].rearrange("p k n -> p (k n)"), p_t_lo)
                if t0 is not None:
                    k = i % 2
                    dve.wait_ge(score_mm, count(*t0))
                    if i == 0:
                        dve.wait_ge(mask_ready, 2 * (b + 1))
                        dve.wait_ge(ln1_pow, b + 1)
                    nc.vector.scalar_tensor_tensor(prob[:, k, :], ps_score[:, :], ln1_rstd[:, i:i + 1], keep[:, :],
                                                   ALU.mult, ALU.mult).then_inc(score_masked, 1)
                    wait_apart(dve, score_masked, count(*t0))
                    nc.vector.tensor_tensor_reduce(prob[:, k, :], prob[:, k, :], fill[:, :], -1.0, 3.0e38, ALU.add, ALU.min,
                                                   neg_max[:, k:k + 1]).then_inc(score_max, 1)
                if t2 is not None:
                    lo(x2_t_hi, count(*t2), x2_t_hl[:, 1].rearrange("p k n -> p (k n)"), x2_t_bank(i)[:, :],
                       x2_t_hl[:, 0].rearrange("p k n -> p (k n)"), x2_t_lo)
                if t3 is not None:
                    lo(tg_t_hi, count(*t3), tg_t_hl[:, 1], p_t_bank(i)[:, 0:P], tg_t_hl[:, 0], tg_t_lo)
                more = tile(b, 0, -NT) is not None
                if t1 is not None:
                    b1, i1 = t1
                    k = i1 % 2
                    dve.wait_ge(exp_done, count(*t1))
                    nc.vector.reciprocal(p_inv[:, k:k + 1], p_sum[:, k:k + 1]).then_inc(p_inverted, 1)
                    if isinstance(b1, int) and t1 == (0, 0):
                        dve.wait_ge(tanh_ready, 1)
                    dve.wait_ge(p_inverted, count(*t1))
                    nc.vector.tensor_scalar(p_scale[:, k:k + 1], p_inv[:, k:k + 1], tanh_g[:, 0:1], None, ALU.mult).then_inc(p_scaled, 1)
                    dve.wait_ge(x_kept, count(*t1))
                    dve.wait_ge(p_scaled, count(*t1))
                    dve.wait_ge(ctx_mm, count(*t1))
                    nc.vector.scalar_tensor_tensor(x2[:, i1, :], ps_ctx[:, :], p_scale[:, k:k + 1], x_res[:, i1, :],
                                                   ALU.mult, ALU.add).then_inc(x2_ready, 1)
                    dve.wait_ge(x2_ready, count(*t1))
                    nc.vector.bn_stats(ln2_stats[:, :], x2[:, i1, :]).then_inc(ln2_stat, 1)
                    wait_apart(dve, ln2_stat, count(*t1))
                    nc.vector.bn_aggr(ln2_mv[:, k, :], ln2_stats[:, :]).then_inc(ln2_aggr, 1)
                    dve.wait_ge(ln2_aggr, count(*t1))
                    nc.vector.tensor_scalar(ln2_ve[:, k:k + 1], ln2_mv[:, k, 1:2], LN_EPS, None, ALU.add).then_inc(ln2_var, 1)
                if t3 is not None:
                    b3, i3 = t3
                    dve.wait_ge(lora_mm, count(*t3))
                    before = tile(b, i, 5)
                    if before is not None:
                        dve.wait_ge(stored[i3 % 2], DMA * (before[0] * (NT // 2) + (before[1] // 2 + 1)))
                    nc.vector.scalar_tensor_tensor(out_sb[:, i3 % 2, :].rearrange("p (h n) -> p h n", h=2),
                                                   ps_ffn[i3 % 2][:, :, 0:HALF], tanh_g[:, 1:2],
                                                   x2[:, i3, :].rearrange("p (h n) -> p h n", h=2),
                                                   ALU.mult, ALU.add).then_inc(out_ready, 1)
                if t1 is not None:
                    k = t1[1] % 2
                    dve.wait_ge(ln2_pow, count(*t1))
                    nc.vector.tensor_scalar(x2n[:, k, :], x2[:, t1[1], :], ln2_mv[:, k, 0:1], ln2_rstd[:, k:k + 1],
                                            ALU.subtract, ALU.mult).then_inc(x2n_ready, 1)
                if t2 is not None:
                    k = t2[1] % 2
                    n0 = N_FFN - HALF - E
                    dve.wait_ge(ffn_mm, count(*t2))
                    nc.vector.tensor_reduce(gate_neg_max[:, k:k + 1], ps_ffn[k][:, 1, n0:n0 + E], AX.X, ALU.max, negate=True).then_inc(gate_max, 1)
                    dve.wait_ge(gate_exped, count(*t2))
                    nc.vector.reciprocal(gate_inv[:, k:k + 1], gate_sum[:, k:k + 1]).then_inc(gate_inverted, 1)
                    dve.wait_ge(gate_inverted, count(*t2))
                    nc.vector.scalar_tensor_tensor(tg[:, k, :].rearrange("p (e r) -> p e r", e=E),
                                                   ps_ffn[k][:, 1, HALF:HALF + ER].rearrange("p (e r) -> p e r", e=E),
                                                   gate_inv[:, k:k + 1],
                                                   gate_exp[:, k, :].rearrange("p (e r) -> p e r", r=1).broadcast_to([P, E, G]),
                                                   ALU.mult, ALU.mult).then_inc(tg_ready, 1)
                if i == 0:
                    for k in values_of(b):
                        v_low(b, k)
                if i in (1, 2) and more:
                    for c in pieces_of(i):
                        x_t_low(b + 1, c)
                    ln1_statistics(b + 1, i - 1)
                if i == 3 and more:
                    make_mask(b + 1)
                    lo(ctx_hi, b + 2, ctx_t_hl[:, 1], ctx_raw[:, :, :], ctx_t_hl[:, 0], ctx_lo)
                    for c in range(C):
                        if c < 2:
                            ln1_statistics(b + 1, 2 + c)
                        q_low(b + 1, c)
                    ln1_variance(b + 1)

            for c in range(C):
                dve.wait_ge(wq_summed, c + 1)
                nc.vector.tensor_scalar(wq_neg_mean[:, c:c + 1], wq_sum[:, c:c + 1], -1.0 / D, None, ALU.mult).then_inc(wq_mean, 1)
                lo(wk_hi, c + 1, wk_hl[:, 1, c, :], wk_raw[:, c, :], wk_hl[:, 0, c, :], wqk_lo)
                dve.wait_ge(wq_hi, c + 1)
                nc.vector.scalar_tensor_tensor(wq_hl[:, 1, c, :], wq_raw[:, c, :], wq_neg_mean[:, c:c + 1], f32(wq_hl[:, 0, c, :]),
                                               ALU.add, ALU.subtract).then_inc(wqk_lo, 1)
            lo(ctx_hi, 1, ctx_t_hl[:, 1], ctx_raw[:, :, :], ctx_t_hl[:, 0], ctx_lo)
            lo(weight_hi, 1, wv_hl[:, 1], stage[:, :].rearrange("p (c n) -> p c n", c=C), wv_hl[:, 0], weight_lo)
            for m in range(C):
                x_t_low(0, m)
                lo(a_hi, m + 1, a_hl[:, 1, m, :], a_bank(m), a_hl[:, 0, m, :], a_lo)
            v_low(0, 0)
            v_low(0, 1)
            for j in range(NT):
                ln1_statistics(0, j)
                q_low(0, j)
            ln1_variance(0)
            make_mask(0)
            lo(weight_hi, 2, ffn_hl[:, 1, :, D:], stage_ffn[:, 0:C * (N_FFN - D)].rearrange("p (c n) -> p c n", c=C),
               ffn_hl[:, 0, :, D:], weight_lo)
            dve.wait_ge(weight_hi, 3)
            nc.vector.scalar_tensor_tensor(lora_v_hl[:, 1], stage_ffn[:, C * (N_FFN - D):], 1.0 / G, f32(lora_v_hl[:, 0]),
                                           ALU.mult, ALU.subtract).then_inc(weight_lo, 1)
            lo(weight_hi, 4, ffn_hl[:, 1, :, 0:D], stage[:, :].rearrange("p (c n) -> p c n", c=C), ffn_hl[:, 0, :, 0:D], weight_lo)
            for i in range(NT):
                step(0, i)
            with dve.Fori(1, B - 1) as b:
                for i in range(NT):
                    step(b, i)
            for i in range(NT + 3):
                step(B - 1, i)


def kernel(x, ctx_1024, mask_BxS2_ik1, g_xattn, g_ffn, L0_xattn_Wq, L0_xattn_Wk, L0_xattn_Wv,
           L0_ffn_weight, L0_ffn_gate_w, L0_ffn_lora_U, L0_ffn_lora_V):
    import numpy as np
    import concourse.bacc as bacc
    from concourse.bass_utils import run_bass_kernel_spmd

    arr = lambda a: np.ascontiguousarray(np.asarray(a))
    E, R, D = L0_ffn_lora_U.shape
    arrays = {
        "x": arr(x),
        "x_t": arr(np.asarray(x).transpose(0, 2, 1)),
        "ctx_t": arr(np.asarray(ctx_1024).transpose(0, 2, 1)),
        "mask": arr(mask_BxS2_ik1),
        "g_xattn": arr(g_xattn),
        "g_ffn": arr(g_ffn),
        "wq": arr(L0_xattn_Wq),
        "wk": arr(L0_xattn_Wk),
        "wv_t": arr(np.asarray(L0_xattn_Wv).T),
        "ffn_t": arr(np.concatenate([np.asarray(L0_ffn_weight), np.asarray(L0_ffn_lora_U).reshape(E * R, D),
                                     np.asarray(L0_ffn_gate_w)]).T),
        "lora_v": arr(np.asarray(L0_ffn_lora_V).transpose(0, 2, 1).reshape(E * R, -1)),
    }
    nc = bacc.Bacc("TRN2", target_bir_lowering=False, num_devices=1)
    args = [nc.dram_tensor(f"in_{n}", a.shape, mybir.dt.from_np(a.dtype), kind="ExternalInput").ap() for n, a in arrays.items()]
    out = nc.dram_tensor("out", arrays["x"].shape, F32, kind="ExternalOutput").ap()
    flamingo_block(nc, *args, out)
    r = run_bass_kernel_spmd(nc, [{f"in_{n}": a for n, a in arrays.items()}], core_ids=[0])
    return r.results[0]["out"]
```

```python
from contextlib import ExitStack

import concourse.bass as bass
from concourse import mybir

F32 = mybir.dt.float32
F32R = mybir.dt.float32r
I32 = mybir.dt.int32
ALU = mybir.AluOpType
ACT = mybir.ActivationFunctionType
AX = mybir.AxisListType

P = 128
MASK_FILL = -99999.0
LN_EPS = 1e-5
DMA = 16


def flamingo_block(nc, x, x_t, ctx_t, mask, g_xattn, g_ffn, wq, wk, wv_t, ffn_t, lora_v, out):
    B, S, D = x.shape
    E, G = 8, 16
    ER = E * G
    C = D // P
    NT = S // P
    N_FFN = D + ER + E
    HALF = D // 2
    TILES = B * NT
    assert S == D == 512 and ER == P and ffn_t.shape[1] == N_FFN and lora_v.shape[0] == ER

    with ExitStack() as stack:
        def sb(name, shape, dt=F32):
            return stack.enter_context(nc.sbuf_tensor(name, shape, dt))

        def psum(name, shape):
            return stack.enter_context(nc.psum_tensor(name, shape, F32))

        def sem(name):
            return stack.enter_context(nc.semaphore(name))

        a_hl = sb("a_hl", [P, 2, C, D], F32R)
        wv_hl = sb("wv_hl", [P, 2, C, D], F32R)
        ffn_hl = sb("ffn_hl", [P, 2, C, N_FFN], F32R)
        lora_v_hl = sb("lora_v_hl", [P, 2, D], F32R)
        x_t_hl = sb("x_t_hl", [P, 2, C, S], F32R)
        q_t_hl = sb("q_t_hl", [P, 2, C, S], F32R)
        ctx_t_hl = sb("ctx_t_hl", [P, 2, C, S], F32R)
        v_hl = sb("v_hl", [P, 2, NT, D], F32R)
        p_t_hl = sb("p_t_hl", [P, 2, NT, P], F32R)
        x2_t_hl = sb("x2_t_hl", [P, 2, C, P], F32R)
        tg_t_hl = sb("tg_t_hl", [P, 2, P], F32R)
        wq_hl, wk_hl = v_hl, q_t_hl

        x_in = sb("x_in", [P, NT, D])
        x_res = sb("x_res", [P, NT, D])
        x_t_raw = sb("x_t_raw", [P, C, S])
        ctx_raw = sb("ctx_raw", [P, C, S])
        mask_raw = sb("mask_raw", [P, S], I32)
        keep = sb("keep", [P, S])
        fill = sb("fill", [P, S])
        prob = sb("prob", [P, 2, S])
        x2 = sb("x2", [P, NT, D])
        x2n = sb("x2n", [P, 2, D])
        out_sb = sb("out_sb", [P, 2, D])
        stage = sb("stage", [P, C * D])
        stage_ffn = sb("stage_ffn", [P, C * (N_FFN - D) + D])
        wq_raw, wk_raw = x2, x_res
        wv_raw = stage[:, :].rearrange("p (c n) -> p c n", c=C)
        wv_halves = [slice(0, C // 2), slice(C // 2, C)]
        wq_neg_sum = sb("wq_neg_sum", [P, C])
        wq_neg_mean = sb("wq_neg_mean", [P, C])
        ident = sb("ident", [P, P])
        minus_half = sb("minus_half", [P, 1])
        gains = sb("gains", [P, 2])
        tanh_g = sb("tanh_g", [P, 2])
        ln1_stats = sb("ln1_stats", [P, NT, 6])
        ln1_mv = sb("ln1_mv", [P, NT, 2])
        ln1_ve = sb("ln1_ve", [P, NT])
        ln1_rstd = sb("ln1_rstd", [P, NT])
        ln2_stats = sb("ln2_stats", [P, 6])
        ln2_mv = sb("ln2_mv", [P, 2, 2])
        ln2_ve = sb("ln2_ve", [P, 2])
        ln2_rstd = sb("ln2_rstd", [P, 2])
        neg_max = sb("neg_max", [P, 2])
        p_sum = sb("p_sum", [P, 2])
        p_inv = sb("p_inv", [P, 2])
        p_scale = sb("p_scale", [P, 2])
        gate_neg_max = sb("gate_neg_max", [P, 2])
        gate_exp = sb("gate_exp", [P, 2, E])
        gate_sum = sb("gate_sum", [P, 2])
        gate_inv = sb("gate_inv", [P, 2])
        tg = sb("tg", [P, 2, P])

        ps_score = psum("ps_score", [P, S])
        ps_ctx = psum("ps_ctx", [P, D])
        ps_work = [psum("ps_work0", [P, 512]), psum("ps_work1", [P, 512])]
        ps_ffn = [psum("ps_ffn0", [P, 2, 512]), psum("ps_ffn1", [P, 2, 512])]

        wq_in = [sem(f"wq_in{c}") for c in range(C)]
        wk_in = [sem(f"wk_in{c}") for c in range(C)]
        wv_in, ffn_in, lora_in, gain_in = map(sem, ("wv_in", "ffn_in", "lora_in", "gain_in"))
        x_loaded = [sem(f"x_loaded{j}") for j in range(NT)]
        x_t_loaded, ctx_loaded, mask_loaded = sem("x_t_loaded"), sem("ctx_loaded"), sem("mask_loaded")
        stored = [sem("stored0"), sem("stored1")]
        waits_passed = sem("waits_passed")
        ident_zeroed, consts_ready = sem("ident_zeroed"), sem("consts_ready")
        tanh_ready = sem("tanh_ready")
        wq_summed, wq_mean = sem("wq_summed"), sem("wq_mean")
        wk_hi, wq_hi, wk_lo, wq_lo = map(sem, ("wk_hi", "wq_hi", "wk_lo", "wq_lo"))
        wv_hi, wv_lo = sem("wv_hi"), sem("wv_lo")
        weight_hi, weight_lo = sem("weight_hi"), sem("weight_lo")
        a_mm, a_hi, a_lo = sem("a_mm"), sem("a_hi"), sem("a_lo")
        v_mm, v_hi, v_lo = sem("v_mm"), sem("v_hi"), sem("v_lo")
        q_mm, q_hi, q_lo = sem("q_mm"), sem("q_hi"), sem("q_lo")
        x_t_hi, x_t_lo = sem("x_t_hi"), sem("x_t_lo")
        ln1_stat, ln1_aggr = sem("ln1_stat"), sem("ln1_aggr")
        x_kept = sem("x_kept")
        ln1_var, ln1_pow = sem("ln1_var"), sem("ln1_pow")
        ctx_hi, ctx_lo, mask_ready = sem("ctx_hi"), sem("ctx_lo"), sem("mask_ready")
        score_mm, score_masked, score_max, exp_done = sem("score_mm"), sem("score_masked"), sem("score_max"), sem("exp_done")
        p_t_mm, p_t_hi, p_t_lo = sem("p_t_mm"), sem("p_t_hi"), sem("p_t_lo")
        p_inverted, p_scaled = sem("p_inverted"), sem("p_scaled")
        ctx_mm, x2_ready = sem("ctx_mm"), sem("x2_ready")
        ln2_stat, ln2_aggr, ln2_var, ln2_pow, x2n_ready = (
            sem("ln2_stat"), sem("ln2_aggr"), sem("ln2_var"), sem("ln2_pow"), sem("x2n_ready"))
        x2_t_mm, x2_t_hi, x2_t_lo = sem("x2_t_mm"), sem("x2_t_hi"), sem("x2_t_lo")
        ffn_mm, gate_max, gate_exped, gate_inverted, tg_ready = (
            sem("ffn_mm"), sem("gate_max"), sem("gate_exped"), sem("gate_inverted"), sem("tg_ready"))
        tg_t_mm, tg_t_hi, tg_t_lo = sem("tg_t_mm"), sem("tg_t_hi"), sem("tg_t_lo")
        lora_mm, out_ready = sem("lora_mm"), sem("out_ready")

        def tile(b, i, back=0):
            b, i = b + (i - back) // NT, (i - back) % NT
            if isinstance(b, int) and not 0 <= b < B:
                return None
            return b, i

        def count(b, i):
            return b * NT + (i + 1)

        def x2_t_bank(i):
            return ps_work[i % 2]

        def tg_t_bank(i):
            return ps_work[(i + 1) % 2]

        def p_t_bank(i):
            return ps_work[i % 2]

        def v_bank(b, k):
            if isinstance(b, int) and b == 0:
                return (ps_score[:, :], ps_ctx[:, :], ps_ffn[0][:, 0, :], ps_ffn[0][:, 1, :])[k]
            return ps_work[(k + 1) % 2][:, :]

        def q_bank(c):
            return ps_work[c % 2][:, :]

        def a_bank(m):
            return ps_ffn[m // 2][:, m % 2, :]

        def values_of(b):
            return (2, 3) if isinstance(b, int) and b == 0 else (0, 1, 2, 3)

        def chunks_of(b, i):
            if tile(b, 0, -NT) is None:
                return ()
            if isinstance(b, int) and b == 0:
                return {0: (0, 1, 2, 3)}.get(i, ())
            return {1: (0, 1), 2: (2, 3)}.get(i, ())

        def statistics_of(b, i):
            if tile(b, 0, -NT) is None:
                return ()
            if isinstance(b, int) and b == 0:
                return {3: (0, 1, 2, 3)}.get(i, ())
            return {1: (0,), 2: (1,), 3: (2, 3)}.get(i, ())

        def is_first(b, i):
            return isinstance(b, int) and (b, i) == (0, 0)

        def f32(ap):
            return ap.bitcast(F32)

        def wait_apart(engine, semaphore, value):
            engine.wait_ge(semaphore, value)
            engine.sem_inc(waits_passed, 1)

        block = stack.enter_context(nc.Block())

        @block.sync
        def _(sp):
            def load_x(b, j):
                sp.dma_start(x_in[:, j, :], x[b, j * P:(j + 1) * P, :]).then_inc(x_loaded[j], DMA)

            def load_x_t(b):
                sp.dma_start(x_t_raw[:, :, :], x_t[b].rearrange("(c p) n -> p c n", p=P)).then_inc(x_t_loaded, DMA)

            def load_ctx(b):
                sp.dma_start(ctx_raw[:, :, :], ctx_t[b].rearrange("(c p) k -> p c k", p=P)).then_inc(ctx_loaded, DMA)

            def load_mask(b):
                sp.dma_start(mask_raw[:, :], mask.rearrange("(b o) s -> b o s", o=1)[b].broadcast_to([P, S])).then_inc(mask_loaded, DMA)

            def step(b, i):
                last = tile(b, i, 3)
                if last is not None:
                    sp.wait_ge(out_ready, count(*last))
                    lb, li = last
                    sp.dma_start(out[lb, li * P:(li + 1) * P, :], out_sb[:, li % 2, :]).then_inc(stored[li % 2], DMA)
                if i == 0 and tile(b, 0, -NT) is not None:
                    sp.wait_ge(x_t_lo, count(b, NT - 1))
                    load_x_t(b + 1)
                    sp.wait_ge(ctx_lo, b + 1)
                    load_ctx(b + 1)
                    sp.wait_ge(mask_ready, 2 * (b + 1))
                    load_mask(b + 1)
                    for j in range(NT):
                        sp.wait_ge(x_kept, count(b, j))
                        sp.wait_ge(ln1_stat, count(b, j))
                        load_x(b + 1, j)

            for c in range(C):
                sp.dma_start(wq_raw[:, c, :], wq[c * P:(c + 1) * P, :]).then_inc(wq_in[c], DMA)
                sp.dma_start(wk_raw[:, c, :], wk[c * P:(c + 1) * P, :]).then_inc(wk_in[c], DMA)
            load_ctx(0)
            sp.dma_start(stage[:, :].rearrange("p (c n) -> p c n", c=C), wv_t.rearrange("(c p) n -> p c n", p=P)).then_inc(wv_in, DMA)
            load_x_t(0)
            load_mask(0)
            for j in range(NT):
                load_x(0, j)
            sp.dma_start(gains[:, 0:1], g_xattn.rearrange("(a n) -> a n", a=1).broadcast_to([P, 1])).then_inc(gain_in, DMA)
            sp.dma_start(gains[:, 1:2], g_ffn.rearrange("(a n) -> a n", a=1).broadcast_to([P, 1])).then_inc(gain_in, DMA)
            sp.dma_start(stage_ffn[:, 0:C * (N_FFN - D)].rearrange("p (c n) -> p c n", c=C),
                         ffn_t[:, D:].rearrange("(c p) n -> p c n", p=P)).then_inc(lora_in, DMA)
            sp.dma_start(stage_ffn[:, C * (N_FFN - D):], lora_v).then_inc(lora_in, DMA)
            sp.wait_ge(wv_lo, len(wv_halves))
            sp.dma_start(stage[:, :].rearrange("p (c n) -> p c n", c=C),
                         ffn_t[:, 0:D].rearrange("(c p) n -> p c n", p=P)).then_inc(ffn_in, DMA)
            for i in range(NT):
                step(0, i)
            with sp.Fori(1, B - 1) as b:
                for i in range(NT):
                    step(b, i)
            for i in range(NT + 3):
                step(B - 1, i)
            for s in range(2):
                sp.wait_ge(stored[s], DMA * TILES // 2)

        @block.gpsimd
        def _(pool):
            def keep_x(b, j):
                if isinstance(b, int) and b == 0:
                    pool.wait_ge(x_loaded[j], DMA)
                else:
                    pool.wait_ge(x_loaded[j], (b + 1) * DMA)
                    wait_apart(pool, x2_ready, count(b - 1, j))
                nc.gpsimd.tensor_copy(x_res[:, j, :], x_in[:, j, :]).then_inc(x_kept, 1)

            def ln1_power(b):
                pool.wait_ge(ln1_var, b + 1)
                if not (isinstance(b, int) and b == 0):
                    pool.wait_ge(score_masked, count(b - 1, NT - 1))
                nc.gpsimd.tensor_tensor(ln1_rstd[:, :], ln1_ve[:, :], minus_half[:, :].broadcast_to([P, NT]), ALU.pow).then_inc(ln1_pow, 1)

            def step(b, i):
                t1 = tile(b, i, 1)
                if t1 is not None:
                    k = t1[1] % 2
                    pool.wait_ge(ln2_var, count(*t1))
                    nc.gpsimd.tensor_tensor(ln2_rstd[:, k:k + 1], ln2_ve[:, k:k + 1], minus_half[:, :], ALU.pow).then_inc(ln2_pow, 1)
                kept = tile(b, i, -(NT - 1))
                if kept is not None and not (isinstance(b, int) and b == 0 and i == 0):
                    keep_x(*kept)
                if i == 3 and tile(b, 0, -NT) is not None:
                    ln1_power(b + 1)

            nc.gpsimd.memset(ident[:, :], 0.0).then_inc(ident_zeroed, 1)
            nc.gpsimd.memset(minus_half[:, :], -0.5).then_inc(consts_ready, 1)
            pool.wait_ge(ident_zeroed, 1)
            nc.gpsimd.affine_select(out=ident[:, :], in_=ident[:, :], compare_op=ALU.not_equal, fill=1.0,
                                    base=0, pattern=[[-1, P]], channel_multiplier=1).then_inc(consts_ready, 1)
            pool.wait_ge(consts_ready, 2)
            pool.wait_ge(wk_lo, C)
            for j in range(NT):
                keep_x(0, j)
            ln1_power(0)
            for i in range(NT):
                step(0, i)
            with pool.Fori(1, B - 1) as b:
                for i in range(NT):
                    step(b, i)
            for i in range(NT + 3):
                step(B - 1, i)

        @block.tensor
        def _(pe):
            def product(bank, lhs, rhs, cols, lhs_cols, k_chunks=C, chunk_wait=None):
                for c in range(k_chunks):
                    if chunk_wait:
                        chunk_wait(c)
                    for l, r in ((0, 0), (0, 1), (1, 0)):
                        mm = pe.matmul(bank, lhs[:, l, c, lhs_cols], rhs[:, r, c, cols],
                                       start=(c == 0 and l == r), stop=(c == k_chunks - 1 and l == 1))
                return mm

            def transposes(bank, tiles):
                for c, ap in enumerate(tiles):
                    mm = pe.transpose(bank[:, c * P:(c + 1) * P], ap, ident[:, :])
                return mm

            def step(b, i):
                t0, t1, t2, t3 = (tile(b, i, d) for d in range(4))
                more = tile(b, 0, -NT) is not None
                if t0 is not None:
                    if i == 0:
                        pe.wait_ge(ctx_lo, b + 1)
                    if t1 is not None:
                        pe.wait_ge(score_masked, count(*t1))
                    product(ps_score[:, :], q_t_hl, ctx_t_hl, slice(0, S), slice(i * P, (i + 1) * P),
                            chunk_wait=(lambda c: pe.wait_ge(q_lo, count(b, c))) if i == 0 else None).then_inc(score_mm, 1)
                if t2 is not None:
                    k = t2[1] % 2
                    t4 = tile(b, i, 4)
                    if i == 0:
                        pe.wait_ge(q_lo, count(b, 2))
                    elif i == 1:
                        pe.wait_ge(v_lo, count(b, 2))
                    elif t4 is not None:
                        pe.wait_ge(tg_t_lo, count(*t4))
                    pe.wait_ge(x2n_ready, count(*t2))
                    transposes(x2_t_bank(i), [x2n[:, k, c * P:(c + 1) * P] for c in range(C)]).then_inc(x2_t_mm, 1)
                if t3 is not None:
                    k = t3[1] % 2
                    if i == 0:
                        pe.wait_ge(q_lo, count(b, 3))
                    elif i == 1:
                        pe.wait_ge(v_lo, count(b, 3))
                    elif t1 is not None:
                        pe.wait_ge(p_t_lo, count(*t1))
                    pe.wait_ge(tg_ready, count(*t3))
                    transposes(tg_t_bank(i), [tg[:, k, :]]).then_inc(tg_t_mm, 1)
                if t1 is not None:
                    pe.wait_ge(p_t_lo, count(*t1))
                    if t1[1] == 0:
                        pe.wait_ge(v_lo, count(t1[0], NT - 1))
                    if t2 is not None:
                        pe.wait_ge(x2_ready, count(*t2))
                    product(ps_ctx[:, :], p_t_hl, v_hl, slice(0, D), slice(0, P)).then_inc(ctx_mm, 1)
                if t3 is not None and t1 is not None:
                    lora(b, i)
                if t0 is not None and not is_first(b, i):
                    p_transposes(b, i)
                if t2 is not None:
                    ffn(b, i, with_lora=t3 is not None and t1 is None)
                elif t3 is not None:
                    lora(b, i)
                if i == 0:
                    for k in values_of(b):
                        if not (isinstance(b, int) and b == 0):
                            if k >= 2:
                                pe.wait_ge(v_lo, count(b, k - 2))
                            else:
                                pe.wait_ge((tg_t_lo, p_t_lo)[k], count(*(t3, t0)[k]))
                        values(b, k)
                if is_first(b, i):
                    p_transposes(b, i)
                if i == 3 and more:
                    pe.wait_ge(x_t_lo, count(b + 1, NT - 1))
                    for c in range(C):
                        if c >= 2:
                            pe.wait_ge(q_lo, count(b + 1, c - 2))
                        else:
                            pe.wait_ge((tg_t_lo, p_t_lo)[c], count(*(t3, t0)[c]))
                        queries(c)

            def lora(b, i):
                t3 = tile(b, i, 3)
                pe.wait_ge(tg_t_lo, count(*t3))
                bank = ps_ffn[t3[1] % 2]
                for l, r in ((0, 0), (0, 1), (1, 0)):
                    for h in range(2):
                        mm = pe.matmul(bank[:, h, 0:HALF], tg_t_hl[:, l, :], lora_v_hl[:, r, h * HALF:(h + 1) * HALF],
                                       start=False, stop=(l == 1), skip_group_check=True)
                mm.then_inc(lora_mm, 1)

            def ffn(b, i, with_lora):
                t2, t4 = tile(b, i, 2), tile(b, i, 4)
                pe.wait_ge(x2_t_lo, count(*t2))
                if isinstance(t2[0], int) and t2 == (0, 0):
                    pe.wait_ge(weight_lo, 2 + C)
                if t4 is not None:
                    pe.wait_ge(out_ready, count(*t4))
                for h, cols in ((1, slice(HALF, N_FFN)), (0, slice(0, HALF))):
                    bank = ps_ffn[t2[1] % 2][:, h, 0:cols.stop - cols.start]
                    mm = product(bank, x2_t_hl, ffn_hl, cols, slice(0, P))
                    if h == 1:
                        mm.then_inc(ffn_mm, 1)
                        if with_lora:
                            lora(b, i)

            def p_transposes(b, i):
                t2 = tile(b, i, 2)
                if t2 is not None:
                    pe.wait_ge(x2_t_lo, count(*t2))
                if is_first(b, i):
                    pe.wait_ge(consts_ready, 2)
                pe.wait_ge(exp_done, count(b, i))
                transposes(p_t_bank(i), [prob[:, i % 2, k * P:(k + 1) * P] for k in range(NT)]).then_inc(p_t_mm, 1)

            def queries(c, chunk_wait=None):
                product(q_bank(c), a_hl, x_t_hl, slice(0, S), slice(c * P, (c + 1) * P),
                        chunk_wait=chunk_wait).then_inc(q_mm, 1)

            def first_queries_wait(c):
                pe.wait_ge(x_t_lo, c + 1)
                pe.wait_ge(a_lo, c + 1)

            def values(b, k, chunk_wait=None):
                product(v_bank(b, k), ctx_t_hl, wv_hl, slice(0, D), slice(k * P, (k + 1) * P),
                        chunk_wait=chunk_wait).then_inc(v_mm, 1)

            def a_pass(c, m, l, r):
                return pe.matmul(a_bank(m), wq_hl[:, l, c, m * P:(m + 1) * P], wk_hl[:, r, c, :],
                                 start=(c == 0 and l == r), stop=(c == C - 1 and l == 1))

            for c in range(C - 1):
                pe.wait_ge(wk_hi, c + 1)
                pe.wait_ge(wq_hi, c + 1)
                for m in range(C):
                    a_pass(c, m, 0, 0)
                pe.wait_ge(wk_lo, c + 1)
                for m in range(C):
                    a_pass(c, m, 0, 1)
                pe.wait_ge(wq_lo, c + 1)
                for m in range(C):
                    a_pass(c, m, 1, 0)
            pe.wait_ge(wk_lo, C)
            pe.wait_ge(wq_lo, C)
            for m in range(C):
                for l, r in ((0, 0), (0, 1), (1, 0)):
                    mm = a_pass(C - 1, m, l, r)
                mm.then_inc(a_mm, 1)
            pe.wait_ge(ctx_lo, 1)
            values(0, 0, chunk_wait=lambda c: pe.wait_ge(wv_lo, 1 + c // (C // 2)))
            values(0, 1)
            for c in range(C):
                if c >= 2:
                    pe.wait_ge(q_lo, c - 1)
                queries(c, chunk_wait=first_queries_wait if c == 0 else None)
            for i in range(NT):
                step(0, i)
            with pe.Fori(1, B - 1) as b:
                for i in range(NT):
                    step(b, i)
            for i in range(NT + 3):
                step(B - 1, i)

        @block.scalar
        def _(act):
            def hi(ready, value, dst, src, done):
                act.wait_ge(ready, value)
                nc.scalar.activation(dst, src, ACT.Copy).then_inc(done, 1)

            def step(b, i):
                t0, t1, t2, t3 = (tile(b, i, d) for d in range(4))
                more = tile(b, 0, -NT) is not None
                if t2 is not None:
                    hi(x2_t_mm, count(*t2), x2_t_hl[:, 0], x2_t_bank(i)[:, :], x2_t_hi)
                if t3 is not None:
                    hi(tg_t_mm, count(*t3), tg_t_hl[:, 0], tg_t_bank(i)[:, 0:P], tg_t_hi)
                if t0 is not None:
                    k = i % 2
                    act.wait_ge(score_max, count(*t0))
                    nc.scalar.activation(prob[:, k, :], prob[:, k, :], ACT.Exp, bias=neg_max[:, k:k + 1], scale=-1.0,
                                         accum_out=p_sum[:, k:k + 1]).then_inc(exp_done, 1)
                if i == 3 and more:
                    act.wait_ge(score_mm, count(b, i))
                    hi(ctx_loaded, (b + 2) * DMA, ctx_t_hl[:, 0], ctx_raw[:, :, :], ctx_hi)
                if not is_first(b, i):
                    for c in chunks_of(b, i):
                        x_t_high(b + 1, c)
                    if t0 is not None:
                        p_t_high(b, i)
                if t2 is not None:
                    k = t2[1] % 2
                    act.wait_ge(gate_max, count(*t2))
                    nc.scalar.activation(gate_exp[:, k, :], ps_ffn[k][:, 1, N_FFN - HALF - E:N_FFN - HALF], ACT.Exp,
                                         bias=gate_neg_max[:, k:k + 1], accum_out=gate_sum[:, k:k + 1]).then_inc(gate_exped, 1)
                if i == 0:
                    for k in values_of(b):
                        v_high(b, k)
                        if is_first(b, i):
                            for c in chunks_of(b, i)[2 * k - 4:2 * k - 2]:
                                x_t_high(b + 1, c)
                if is_first(b, i):
                    p_t_high(b, i)
                if i == 3 and more:
                    for c in range(C):
                        q_high(b + 1, c)

            def p_t_high(b, i):
                hi(p_t_mm, count(b, i), p_t_hl[:, 0], p_t_bank(i)[:, :], p_t_hi)

            def v_high(b, k):
                hi(v_mm, count(b, k), v_hl[:, 0, k, :], v_bank(b, k), v_hi)

            def x_t_high(b, c):
                if c == 0 and not (isinstance(b, int) and b == 0):
                    act.wait_ge(q_mm, count(b - 1, C - 1))
                hi(x_t_loaded, (b + 1) * DMA, x_t_hl[:, 0, c, :], x_t_raw[:, c, :], x_t_hi)

            def q_high(b, c):
                hi(q_mm, count(b, c), q_t_hl[:, 0, c, :], q_bank(c), q_hi)

            for c in range(C):
                hi(wk_in[c], DMA, wk_hl[:, 0, c, :], wk_raw[:, c, :], wk_hi)
                act.wait_ge(wq_mean, c + 1)
                nc.scalar.activation(wq_hl[:, 0, c, :], wq_raw[:, c, :], ACT.Identity, bias=wq_neg_mean[:, c:c + 1]).then_inc(wq_hi, 1)
            hi(ctx_loaded, DMA, ctx_t_hl[:, 0], ctx_raw[:, :, :], ctx_hi)
            for h in wv_halves:
                hi(wv_in, DMA, wv_hl[:, 0, h, :], wv_raw[:, h, :], wv_hi)
            for c in range(C):
                x_t_high(0, c)
            for m in range(C):
                hi(a_mm, m + 1, a_hl[:, 0, m, :], a_bank(m), a_hi)
            v_high(0, 0)
            v_high(0, 1)
            act.wait_ge(gain_in, 2 * DMA)
            nc.scalar.activation(tanh_g[:, :], gains[:, :], ACT.Tanh).then_inc(tanh_ready, 1)
            hi(lora_in, 2 * DMA, ffn_hl[:, 0, :, D:], stage_ffn[:, 0:C * (N_FFN - D)].rearrange("p (c n) -> p c n", c=C), weight_hi)
            nc.scalar.activation(lora_v_hl[:, 0], stage_ffn[:, C * (N_FFN - D):], ACT.Copy, scale=1.0 / G).then_inc(weight_hi, 1)
            hi(ffn_in, DMA, ffn_hl[:, 0, :, 0:D], stage[:, :].rearrange("p (c n) -> p c n", c=C), weight_hi)
            for c in range(C):
                q_high(0, c)
            for i in range(NT):
                step(0, i)
            with act.Fori(1, B - 1) as b:
                for i in range(NT):
                    step(b, i)
            for i in range(NT + 3):
                step(B - 1, i)

        @block.vector
        def _(dve):
            def lo(ready, value, dst, src, high, done):
                dve.wait_ge(ready, value)
                nc.vector.tensor_tensor(dst, src, f32(high), ALU.subtract).then_inc(done, 1)

            def make_mask(b):
                dve.wait_ge(mask_loaded, (b + 1) * DMA)
                nc.vector.tensor_scalar(keep[:, :], mask_raw[:, :], 0, None, ALU.not_equal).then_inc(mask_ready, 1)
                nc.vector.tensor_scalar(fill[:, :], mask_raw[:, :], 0, MASK_FILL, ALU.is_equal, ALU.mult).then_inc(mask_ready, 1)

            def ln1_statistics(b, j):
                dve.wait_ge(x_loaded[j], (b + 1) * DMA)
                nc.vector.bn_stats(ln1_stats[:, j, :], x_in[:, j, :]).then_inc(ln1_stat, 1)
                wait_apart(dve, ln1_stat, count(b, j))
                nc.vector.bn_aggr(ln1_mv[:, j, :], ln1_stats[:, j, :]).then_inc(ln1_aggr, 1)

            def ln1_variance(b):
                dve.wait_ge(ln1_aggr, count(b, NT - 1))
                nc.vector.tensor_scalar(ln1_ve[:, :], ln1_mv[:, :, 1], LN_EPS, None, ALU.add).then_inc(ln1_var, 1)

            def x_t_low(b, c):
                lo(x_t_hi, count(b, c), x_t_hl[:, 1, c, :], x_t_raw[:, c, :], x_t_hl[:, 0, c, :], x_t_lo)

            def output(b, i):
                t3 = tile(b, i, 3)
                b3, i3 = t3
                dve.wait_ge(lora_mm, count(*t3))
                before = tile(b, i, 5)
                if before is not None:
                    dve.wait_ge(stored[i3 % 2], DMA * (before[0] * (NT // 2) + (before[1] // 2 + 1)))
                nc.vector.scalar_tensor_tensor(out_sb[:, i3 % 2, :].rearrange("p (h n) -> p h n", h=2),
                                               ps_ffn[i3 % 2][:, :, 0:HALF], tanh_g[:, 1:2],
                                               x2[:, i3, :].rearrange("p (h n) -> p h n", h=2),
                                               ALU.mult, ALU.add).then_inc(out_ready, 1)

            def gates(b2, i2):
                k = i2 % 2
                n0 = N_FFN - HALF - E
                dve.wait_ge(ffn_mm, count(b2, i2))
                nc.vector.tensor_reduce(gate_neg_max[:, k:k + 1], ps_ffn[k][:, 1, n0:n0 + E], AX.X, ALU.max, negate=True).then_inc(gate_max, 1)
                dve.wait_ge(gate_exped, count(b2, i2))
                nc.vector.reciprocal(gate_inv[:, k:k + 1], gate_sum[:, k:k + 1]).then_inc(gate_inverted, 1)
                dve.wait_ge(gate_inverted, count(b2, i2))
                nc.vector.scalar_tensor_tensor(tg[:, k, :].rearrange("p (e r) -> p e r", e=E),
                                               ps_ffn[k][:, 1, HALF:HALF + ER].rearrange("p (e r) -> p e r", e=E),
                                               gate_inv[:, k:k + 1],
                                               gate_exp[:, k, :].rearrange("p (e r) -> p e r", r=1).broadcast_to([P, E, G]),
                                               ALU.mult, ALU.mult).then_inc(tg_ready, 1)

            def p_t_low(b, i):
                lo(p_t_hi, count(b, i), p_t_hl[:, 1].rearrange("p k n -> p (k n)"), p_t_bank(i)[:, :],
                   p_t_hl[:, 0].rearrange("p k n -> p (k n)"), p_t_lo)

            def v_low(b, k):
                lo(v_hi, count(b, k), v_hl[:, 1, k, :], v_bank(b, k), v_hl[:, 0, k, :], v_lo)

            def q_low(b, c):
                lo(q_hi, count(b, c), q_t_hl[:, 1, c, :], q_bank(c), q_t_hl[:, 0, c, :], q_lo)

            def step(b, i):
                t0, t1, t2, t3 = (tile(b, i, d) for d in range(4))
                if t0 is not None:
                    k = i % 2
                    dve.wait_ge(score_mm, count(*t0))
                    if i == 0:
                        dve.wait_ge(mask_ready, 2 * (b + 1))
                        dve.wait_ge(ln1_pow, b + 1)
                    nc.vector.scalar_tensor_tensor(prob[:, k, :], ps_score[:, :], ln1_rstd[:, i:i + 1], keep[:, :],
                                                   ALU.mult, ALU.mult).then_inc(score_masked, 1)
                    wait_apart(dve, score_masked, count(*t0))
                    nc.vector.tensor_tensor_reduce(prob[:, k, :], prob[:, k, :], fill[:, :], -1.0, 3.0e38, ALU.add, ALU.min,
                                                   neg_max[:, k:k + 1]).then_inc(score_max, 1)
                if t2 is not None:
                    lo(x2_t_hi, count(*t2), x2_t_hl[:, 1].rearrange("p k n -> p (k n)"), x2_t_bank(i)[:, :],
                       x2_t_hl[:, 0].rearrange("p k n -> p (k n)"), x2_t_lo)
                if t3 is not None:
                    lo(tg_t_hi, count(*t3), tg_t_hl[:, 1], tg_t_bank(i)[:, 0:P], tg_t_hl[:, 0], tg_t_lo)
                more = tile(b, 0, -NT) is not None
                if t1 is not None:
                    b1, i1 = t1
                    k = i1 % 2
                    dve.wait_ge(exp_done, count(*t1))
                    nc.vector.reciprocal(p_inv[:, k:k + 1], p_sum[:, k:k + 1]).then_inc(p_inverted, 1)
                    if isinstance(b1, int) and t1 == (0, 0):
                        dve.wait_ge(tanh_ready, 1)
                    dve.wait_ge(p_inverted, count(*t1))
                    nc.vector.tensor_scalar(p_scale[:, k:k + 1], p_inv[:, k:k + 1], tanh_g[:, 0:1], None, ALU.mult).then_inc(p_scaled, 1)
                    dve.wait_ge(x_kept, count(*t1))
                    dve.wait_ge(p_scaled, count(*t1))
                    dve.wait_ge(ctx_mm, count(*t1))
                    nc.vector.scalar_tensor_tensor(x2[:, i1, :], ps_ctx[:, :], p_scale[:, k:k + 1], x_res[:, i1, :],
                                                   ALU.mult, ALU.add).then_inc(x2_ready, 1)
                    dve.wait_ge(x2_ready, count(*t1))
                    nc.vector.bn_stats(ln2_stats[:, :], x2[:, i1, :]).then_inc(ln2_stat, 1)
                    wait_apart(dve, ln2_stat, count(*t1))
                    nc.vector.bn_aggr(ln2_mv[:, k, :], ln2_stats[:, :]).then_inc(ln2_aggr, 1)
                    dve.wait_ge(ln2_aggr, count(*t1))
                    nc.vector.tensor_scalar(ln2_ve[:, k:k + 1], ln2_mv[:, k, 1:2], LN_EPS, None, ALU.add).then_inc(ln2_var, 1)
                if t3 is not None and t1 is not None:
                    output(b, i)
                if t1 is not None:
                    k = t1[1] % 2
                    dve.wait_ge(ln2_pow, count(*t1))
                    nc.vector.tensor_scalar(x2n[:, k, :], x2[:, t1[1], :], ln2_mv[:, k, 0:1], ln2_rstd[:, k:k + 1],
                                            ALU.subtract, ALU.mult).then_inc(x2n_ready, 1)
                if t0 is not None and not is_first(b, i):
                    p_t_low(b, i)
                if t2 is not None:
                    gates(*t2)
                if t3 is not None and t1 is None:
                    output(b, i)
                if i == 0:
                    for k in values_of(b):
                        v_low(b, k)
                        if is_first(b, i):
                            for c in chunks_of(b, i)[2 * k - 4:2 * k - 2]:
                                x_t_low(b + 1, c)
                if is_first(b, i):
                    p_t_low(b, i)
                else:
                    for c in chunks_of(b, i):
                        x_t_low(b + 1, c)
                if i < 3:
                    for j in statistics_of(b, i):
                        ln1_statistics(b + 1, j)
                if i == 3 and more:
                    make_mask(b + 1)
                    lo(ctx_hi, b + 2, ctx_t_hl[:, 1], ctx_raw[:, :, :], ctx_t_hl[:, 0], ctx_lo)
                    for c in range(C):
                        for j in statistics_of(b, i)[c:c + 1]:
                            ln1_statistics(b + 1, j)
                        q_low(b + 1, c)
                    ln1_variance(b + 1)

            for c in range(C):
                dve.wait_ge(wq_in[c], DMA)
                nc.vector.tensor_reduce(wq_neg_sum[:, c:c + 1], wq_raw[:, c, :], AX.X, ALU.add, negate=True).then_inc(wq_summed, 1)
                dve.wait_ge(wq_summed, c + 1)
                nc.vector.tensor_scalar(wq_neg_mean[:, c:c + 1], wq_neg_sum[:, c:c + 1], 1.0 / D, None, ALU.mult).then_inc(wq_mean, 1)
                lo(wk_hi, c + 1, wk_hl[:, 1, c, :], wk_raw[:, c, :], wk_hl[:, 0, c, :], wk_lo)
                dve.wait_ge(wq_hi, c + 1)
                nc.vector.scalar_tensor_tensor(wq_hl[:, 1, c, :], wq_raw[:, c, :], wq_neg_mean[:, c:c + 1], f32(wq_hl[:, 0, c, :]),
                                               ALU.add, ALU.subtract).then_inc(wq_lo, 1)
            lo(ctx_hi, 1, ctx_t_hl[:, 1], ctx_raw[:, :, :], ctx_t_hl[:, 0], ctx_lo)
            for n, h in enumerate(wv_halves):
                lo(wv_hi, n + 1, wv_hl[:, 1, h, :], wv_raw[:, h, :], wv_hl[:, 0, h, :], wv_lo)
            for m in range(C):
                x_t_low(0, m)
                lo(a_hi, m + 1, a_hl[:, 1, m, :], a_bank(m), a_hl[:, 0, m, :], a_lo)
            v_low(0, 0)
            v_low(0, 1)
            lo(weight_hi, 1, ffn_hl[:, 1, :, D:], stage_ffn[:, 0:C * (N_FFN - D)].rearrange("p (c n) -> p c n", c=C),
               ffn_hl[:, 0, :, D:], weight_lo)
            dve.wait_ge(weight_hi, 2)
            nc.vector.scalar_tensor_tensor(lora_v_hl[:, 1], stage_ffn[:, C * (N_FFN - D):], 1.0 / G, f32(lora_v_hl[:, 0]),
                                           ALU.mult, ALU.subtract).then_inc(weight_lo, 1)
            make_mask(0)
            ln1_statistics(0, 0)
            for c in range(C):
                q_low(0, c)
                if c + 1 < C:
                    ln1_statistics(0, c + 1)
                lo(weight_hi, 3, ffn_hl[:, 1, c, 0:D], stage[:, c * D:(c + 1) * D], ffn_hl[:, 0, c, 0:D], weight_lo)
            ln1_variance(0)
            for i in range(NT):
                step(0, i)
            with dve.Fori(1, B - 1) as b:
                for i in range(NT):
                    step(b, i)
            for i in range(NT + 3):
                step(B - 1, i)


def kernel(x, ctx_1024, mask_BxS2_ik1, g_xattn, g_ffn, L0_xattn_Wq, L0_xattn_Wk, L0_xattn_Wv,
           L0_ffn_weight, L0_ffn_gate_w, L0_ffn_lora_U, L0_ffn_lora_V):
    import numpy as np
    import concourse.bacc as bacc
    from concourse.bass_utils import run_bass_kernel_spmd

    arr = lambda a: np.ascontiguousarray(np.asarray(a))
    E, R, D = L0_ffn_lora_U.shape
    arrays = {
        "x": arr(x),
        "x_t": arr(np.asarray(x).transpose(0, 2, 1)),
        "ctx_t": arr(np.asarray(ctx_1024).transpose(0, 2, 1)),
        "mask": arr(mask_BxS2_ik1),
        "g_xattn": arr(g_xattn),
        "g_ffn": arr(g_ffn),
        "wq": arr(L0_xattn_Wq),
        "wk": arr(L0_xattn_Wk),
        "wv_t": arr(np.asarray(L0_xattn_Wv).T),
        "ffn_t": arr(np.concatenate([np.asarray(L0_ffn_weight), np.asarray(L0_ffn_lora_U).reshape(E * R, D),
                                     np.asarray(L0_ffn_gate_w)]).T),
        "lora_v": arr(np.asarray(L0_ffn_lora_V).transpose(0, 2, 1).reshape(E * R, -1)),
    }
    nc = bacc.Bacc("TRN2", target_bir_lowering=False, num_devices=1)
    args = [nc.dram_tensor(f"in_{n}", a.shape, mybir.dt.from_np(a.dtype), kind="ExternalInput").ap() for n, a in arrays.items()]
    out = nc.dram_tensor("out", arrays["x"].shape, F32, kind="ExternalOutput").ap()
    flamingo_block(nc, *args, out)
    r = run_bass_kernel_spmd(nc, [{f"in_{n}": a for n, a in arrays.items()}], core_ids=[0])
    return r.results[0]["out"]
```
